# Optimizing a Trainium2 kernel written in Bass

```python
import numpy as np
import jax
import jax.numpy as jnp

def _softmax(x, axis=-1):
    return jax.nn.softmax(x, axis=axis)

def _gelu(x):
    return jax.nn.gelu(x, approximate=True)

def _silu(x):
    return jax.nn.silu(x)

def _sigmoid(x):
    return jax.nn.sigmoid(x)

def _layernorm(x, axis=-1, eps=1e-05):
    m = jnp.mean(x, axis=axis, keepdims=True)
    v = jnp.var(x, axis=axis, keepdims=True)
    return (x - m) / jnp.sqrt(v + eps)

def _scatter_add(tgt, idx, src, axis=0):
    return tgt.at[idx].add(src)

def _segment_sum(src, seg, n):
    return jax.ops.segment_sum(src, seg, n)
kernel_name = 'mk_seq_postln_d1_jaxref_r4_b1a3d0'

def setup_inputs(seed: int=0):
    np.random.seed(seed)
    _w = jnp.asarray

    def _L0_attn_setup():
        import jax, jax.numpy as jnp
        import numpy as np
        from jax import lax
        B, L, D_MODEL = (2, 1024, 256)
        D_STATE, D_CONV, EXPAND = (16, 4, 2)
        D_INNER = D_MODEL * EXPAND
        DT_RANK = (D_MODEL + 15) // 16
        EPS = 1e-05

        def _dt_bias(k):
            u = jax.random.uniform(k, (D_INNER,), dtype=jnp.float32)
            dt = jnp.exp(u * (np.log(0.1) - np.log(0.001)) + np.log(0.001))
            dt = jnp.clip(dt, 0.0001)
            return dt + jnp.log(-jnp.expm1(-dt))

        def _init_A_log():
            a = jnp.arange(1, D_STATE + 1, dtype=jnp.float32)
            return jnp.log(jnp.broadcast_to(a[None, :], (D_INNER, D_STATE)))

        def _causal_dwconv(x, w, b):
            xc = lax.conv_general_dilated(x.transpose(0, 2, 1), w, (1,), [(D_CONV - 1, 0)], dimension_numbers=('NCH', 'OIH', 'NCH'), feature_group_count=D_INNER)
            return (xc + b[None, :, None]).transpose(0, 2, 1)

        def _mamba_dir(xi, z, conv_w, conv_b, xproj_w, dtproj_w, dtproj_b, A_log, Dp):
            xc = jax.nn.silu(_causal_dwconv(xi, conv_w, conv_b))
            x_dbl = jnp.einsum('bld,ed->ble', xc, xproj_w)
            dt = x_dbl[..., :DT_RANK]
            Bm = x_dbl[..., DT_RANK:DT_RANK + D_STATE]
            Cm = x_dbl[..., DT_RANK + D_STATE:]
            delta = jax.nn.softplus(jnp.einsum('blr,dr->bld', dt, dtproj_w) + dtproj_b)
            A = -jnp.exp(A_log)

            def step(h, inp):
                xt, dlt, bt, ct = inp
                h = jnp.exp(dlt[:, :, None] * A) * h + (dlt * xt)[:, :, None] * bt[:, None, :]
                return (h, jnp.einsum('bdn,bn->bd', h, ct))
            h0 = jnp.zeros((xc.shape[0], D_INNER, D_STATE), xc.dtype)
            xs = (xc.transpose(1, 0, 2), delta.transpose(1, 0, 2), Bm.transpose(1, 0, 2), Cm.transpose(1, 0, 2))
            _, ys = lax.scan(step, h0, xs)
            y = ys.transpose(1, 0, 2) + Dp * xc
            return y * jax.nn.silu(z)
        key = jax.random.key(seed)
        ks = jax.random.split(key, 16)

        def g(i, shape, scale=0.02):
            return jax.random.normal(ks[i], shape, dtype=jnp.float32) * scale
        return {'x': jax.random.normal(ks[0], (B, L, D_MODEL), dtype=jnp.float32), 'norm_w': jnp.ones((D_MODEL,), jnp.float32), 'in_proj_w': g(1, (2 * D_INNER, D_MODEL)), 'out_proj_w': g(2, (D_MODEL, D_INNER)), 'conv_w_f': g(3, (D_INNER, 1, D_CONV), 0.1), 'conv_b_f': jnp.zeros((D_INNER,), jnp.float32), 'xproj_w_f': g(4, (DT_RANK + 2 * D_STATE, D_INNER)), 'dtproj_w_f': g(5, (D_INNER, DT_RANK), 0.1), 'dtproj_b_f': _dt_bias(ks[6]), 'A_log_f': _init_A_log(), 'D_f': jnp.ones((D_INNER,), jnp.float32), 'conv_w_b': g(7, (D_INNER, 1, D_CONV), 0.1), 'conv_b_b': jnp.zeros((D_INNER,), jnp.float32), 'xproj_w_b': g(8, (DT_RANK + 2 * D_STATE, D_INNER)), 'dtproj_w_b': g(9, (D_INNER, DT_RANK), 0.1), 'dtproj_b_b': _dt_bias(ks[10]), 'A_log_b': _init_A_log(), 'D_b': jnp.ones((D_INNER,), jnp.float32)}
    _L0_attn_in = _L0_attn_setup()

    def _L0_ffn_setup():
        import jax, jax.numpy as jnp
        import numpy as np
        NUM_TRUE = 8
        NUM_NULL = 2
        NUM_EXPERTS = NUM_TRUE + NUM_NULL
        TOP_K = 2
        key = jax.random.key(seed)
        k0, k1, k2 = jax.random.split(key, 3)
        B, S, D = (4, 512, 256)
        inputs = jax.random.normal(k0, (B, S, D), dtype=jnp.float32)
        gate_w = jax.random.normal(k1, (NUM_EXPERTS, D), dtype=jnp.float32) * 0.02
        gate_b = jnp.zeros((NUM_EXPERTS,), dtype=jnp.float32)
        expert_w = jax.random.normal(k2, (NUM_TRUE, D, D), dtype=jnp.float32) * 0.02
        expert_b = jnp.zeros((NUM_TRUE, D), dtype=jnp.float32)
        return {'inputs': inputs, 'gate_w': gate_w, 'gate_b': gate_b, 'expert_w': expert_w, 'expert_b': expert_b}
    _L0_ffn_in = _L0_ffn_setup()
    _d = {'L0_attn_x': _L0_attn_in['x'], 'L0_attn_norm_w': _L0_attn_in['norm_w'], 'L0_attn_in_proj_w': _L0_attn_in['in_proj_w'], 'L0_attn_out_proj_w': _L0_attn_in['out_proj_w'], 'L0_attn_conv_w_f': _L0_attn_in['conv_w_f'], 'L0_attn_conv_b_f': _L0_attn_in['conv_b_f'], 'L0_attn_xproj_w_f': _L0_attn_in['xproj_w_f'], 'L0_attn_dtproj_w_f': _L0_attn_in['dtproj_w_f'], 'L0_attn_dtproj_b_f': _L0_attn_in['dtproj_b_f'], 'L0_attn_A_log_f': _L0_attn_in['A_log_f'], 'L0_attn_D_f': _L0_attn_in['D_f'], 'L0_attn_conv_w_b': _L0_attn_in['conv_w_b'], 'L0_attn_conv_b_b': _L0_attn_in['conv_b_b'], 'L0_attn_xproj_w_b': _L0_attn_in['xproj_w_b'], 'L0_attn_dtproj_w_b': _L0_attn_in['dtproj_w_b'], 'L0_attn_dtproj_b_b': _L0_attn_in['dtproj_b_b'], 'L0_attn_A_log_b': _L0_attn_in['A_log_b'], 'L0_attn_D_b': _L0_attn_in['D_b'], 'L0_ffn_gate_w': _L0_ffn_in['gate_w'], 'L0_ffn_gate_b': _L0_ffn_in['gate_b'], 'L0_ffn_expert_w': _L0_ffn_in['expert_w'], 'L0_ffn_expert_b': _L0_ffn_in['expert_b']}
    _x0 = _d['L0_attn_x']
    _d['L0_attn_x'] = jax.random.normal(jax.random.fold_in(jax.random.key(seed), 1), (4, 2048, 256), dtype=_x0.dtype)
    del _x0
    return _d

def reference(L0_attn_x, L0_attn_norm_w, L0_attn_in_proj_w, L0_attn_out_proj_w, L0_attn_conv_w_f, L0_attn_conv_b_f, L0_attn_xproj_w_f, L0_attn_dtproj_w_f, L0_attn_dtproj_b_f, L0_attn_A_log_f, L0_attn_D_f, L0_attn_conv_w_b, L0_attn_conv_b_b, L0_attn_xproj_w_b, L0_attn_dtproj_w_b, L0_attn_dtproj_b_b, L0_attn_A_log_b, L0_attn_D_b, L0_ffn_gate_w, L0_ffn_gate_b, L0_ffn_expert_w, L0_ffn_expert_b):

    def _L0_attn_ref(x, norm_w, in_proj_w, out_proj_w, conv_w_f, conv_b_f, xproj_w_f, dtproj_w_f, dtproj_b_f, A_log_f, D_f, conv_w_b, conv_b_b, xproj_w_b, dtproj_w_b, dtproj_b_b, A_log_b, D_b):
        import jax, jax.numpy as jnp
        import numpy as np
        from jax import lax
        B, L, D_MODEL = (2, 1024, 256)
        D_STATE, D_CONV, EXPAND = (16, 4, 2)
        D_INNER = D_MODEL * EXPAND
        DT_RANK = (D_MODEL + 15) // 16
        EPS = 1e-05

        def _dt_bias(k):
            u = jax.random.uniform(k, (D_INNER,), dtype=jnp.float32)
            dt = jnp.exp(u * (np.log(0.1) - np.log(0.001)) + np.log(0.001))
            dt = jnp.clip(dt, 0.0001)
            return dt + jnp.log(-jnp.expm1(-dt))

        def _init_A_log():
            a = jnp.arange(1, D_STATE + 1, dtype=jnp.float32)
            return jnp.log(jnp.broadcast_to(a[None, :], (D_INNER, D_STATE)))

        def _causal_dwconv(x, w, b):
            xc = lax.conv_general_dilated(x.transpose(0, 2, 1), w, (1,), [(D_CONV - 1, 0)], dimension_numbers=('NCH', 'OIH', 'NCH'), feature_group_count=D_INNER)
            return (xc + b[None, :, None]).transpose(0, 2, 1)

        def _mamba_dir(xi, z, conv_w, conv_b, xproj_w, dtproj_w, dtproj_b, A_log, Dp):
            xc = jax.nn.silu(_causal_dwconv(xi, conv_w, conv_b))
            x_dbl = jnp.einsum('bld,ed->ble', xc, xproj_w)
            dt = x_dbl[..., :DT_RANK]
            Bm = x_dbl[..., DT_RANK:DT_RANK + D_STATE]
            Cm = x_dbl[..., DT_RANK + D_STATE:]
            delta = jax.nn.softplus(jnp.einsum('blr,dr->bld', dt, dtproj_w) + dtproj_b)
            A = -jnp.exp(A_log)

            def step(h, inp):
                xt, dlt, bt, ct = inp
                h = jnp.exp(dlt[:, :, None] * A) * h + (dlt * xt)[:, :, None] * bt[:, None, :]
                return (h, jnp.einsum('bdn,bn->bd', h, ct))
            h0 = jnp.zeros((xc.shape[0], D_INNER, D_STATE), xc.dtype)
            xs = (xc.transpose(1, 0, 2), delta.transpose(1, 0, 2), Bm.transpose(1, 0, 2), Cm.transpose(1, 0, 2))
            _, ys = lax.scan(step, h0, xs)
            y = ys.transpose(1, 0, 2) + Dp * xc
            return y * jax.nn.silu(z)
        residual = x
        xn = x * lax.rsqrt(jnp.mean(x * x, axis=-1, keepdims=True) + EPS) * norm_w
        xz = jnp.einsum('bld,ed->ble', xn, in_proj_w)
        xi, z = (xz[..., :D_INNER], xz[..., D_INNER:])
        y_f = _mamba_dir(xi, z, conv_w_f, conv_b_f, xproj_w_f, dtproj_w_f, dtproj_b_f, A_log_f, D_f)
        y_b = _mamba_dir(xi[:, ::-1], z[:, ::-1], conv_w_b, conv_b_b, xproj_w_b, dtproj_w_b, dtproj_b_b, A_log_b, D_b)
        y = 0.5 * y_f + 0.5 * y_b[:, ::-1]
        return jnp.einsum('bld,ed->ble', y, out_proj_w) + residual

    def _L0_ffn_ref(inputs, gate_w, gate_b, expert_w, expert_b):
        import jax, jax.numpy as jnp
        import numpy as np
        NUM_TRUE = 8
        NUM_NULL = 2
        NUM_EXPERTS = NUM_TRUE + NUM_NULL
        TOP_K = 2
        D = inputs.shape[-1]
        x = inputs.reshape(-1, D)
        gate_logits = x @ gate_w.T + gate_b
        gate_probs = jax.nn.softmax(gate_logits, axis=-1)
        weights, selected = jax.lax.top_k(gate_probs, TOP_K)
        true_mask = selected < NUM_TRUE
        true_weights = weights * true_mask
        denom = true_weights.sum(axis=-1, keepdims=True)
        denom = jnp.where(denom > 0, denom, jnp.ones_like(denom))
        norm_w = (true_weights / denom).astype(x.dtype)
        one_hot = jax.nn.one_hot(selected, NUM_EXPERTS, dtype=norm_w.dtype)
        combine_w = jnp.einsum('tk,tke->te', norm_w, one_hot)[:, :NUM_TRUE]
        expert_out = jnp.einsum('td,edh->teh', x, expert_w) + expert_b[None, :, :]
        out = jnp.einsum('te,teh->th', combine_w, expert_out)
        return out.reshape(inputs.shape[:-1] + (out.shape[-1],))
    x = L0_attn_x
    x = _layernorm(x + _L0_attn_ref(x, L0_attn_norm_w, L0_attn_in_proj_w, L0_attn_out_proj_w, L0_attn_conv_w_f, L0_attn_conv_b_f, L0_attn_xproj_w_f, L0_attn_dtproj_w_f, L0_attn_dtproj_b_f, L0_attn_A_log_f, L0_attn_D_f, L0_attn_conv_w_b, L0_attn_conv_b_b, L0_attn_xproj_w_b, L0_attn_dtproj_w_b, L0_attn_dtproj_b_b, L0_attn_A_log_b, L0_attn_D_b), axis=-1)
    x = _layernorm(x + _L0_ffn_ref(x, L0_ffn_gate_w, L0_ffn_gate_b, L0_ffn_expert_w, L0_ffn_expert_b), axis=-1)
    return x

_drawn_inputs = setup_inputs


def setup_inputs(seed=0):
    import zlib

    import numpy as np

    out = dict(_drawn_inputs(seed))
    spreads = {'L0_attn_norm_w': (1.0, 0.6),
     'L0_attn_conv_b_f': (0.0, 0.8),
     'L0_attn_D_f': (1.0, 0.6),
     'L0_attn_conv_b_b': (0.0, 0.8),
     'L0_attn_D_b': (1.0, 0.6),
     'L0_ffn_gate_b': (0.0, 0.1),
     'L0_ffn_expert_b': (0.0, 0.1)}
    factors = {'L0_attn_in_proj_w': 7.187,
     'L0_attn_out_proj_w': 6.538,
     'L0_attn_conv_w_f': 8.0,
     'L0_attn_xproj_w_f': 8.0,
     'L0_attn_dtproj_w_f': 8.0,
     'L0_attn_dtproj_b_f': 8.0,
     'L0_attn_A_log_f': 8.0,
     'L0_attn_conv_w_b': 8.0,
     'L0_attn_xproj_w_b': 8.0,
     'L0_attn_dtproj_w_b': 8.0,
     'L0_attn_dtproj_b_b': 8.0,
     'L0_attn_A_log_b': 8.0}
    for name, (base, spread) in spreads.items():
        noise = np.random.default_rng([zlib.crc32(name.encode()), seed]).standard_normal(out[name].shape)
        drawn = base * np.exp(spread * noise) if base else spread * noise
        out[name] = jnp.asarray(drawn.astype(out[name].dtype))
    for name, factor in factors.items():
        out[name] = (out[name] * factor).astype(out[name].dtype)
    return out
```

```python
import concourse.bass as bass
from concourse import mybir
from contextlib import ExitStack

B, L, DM = 4, 2048, 256
DI, NS, TAPS, RANK = 512, 16, 4, 16
P = 128
T = 512
NCH = B * L // T
CPB = L // T
CT = DI // P
TT = T // P
KC = DM // P
HALO = TAPS - 1
SEG = T + 2
NE, NR = 8, 10
EPS = 1e-5
HUGE = 3.0e38
SERIES_A, SERIES_B, SERIES_C = 3 ** -0.5, -(3 ** 0.5) / 4, 13 / 16
LOG_MARGIN = 8e-8
ON_DVE = (12, 14)
RING = 4
LAG = 3
N_DVE, N_POOL = len(ON_DVE), NS - len(ON_DVE)


def before(n, on_dve):
    return sum((m in ON_DVE) == on_dve for m in range(n))


def wait(eng, sem, value):
    if not isinstance(value, int) or value > 0:
        eng.wait_ge(sem, value)


def hold(eng, sem, value, spare):
    eng.wait_ge(sem, value)
    eng.sem_inc(spare, 1)


def rank_of_backward(i):
    return (i & (NCH - CPB)) + (CPB - 1 - (i & (CPB - 1)))


def mamba_moe(nc, x, in_w, out_w, norm_w, conv_w, conv_b, xproj_w, dt_w, dt_b, a_log, d_skip,
              gate_w, gate_b, expert_w, expert_b, out):
    fp32, bf16 = mybir.dt.float32, mybir.dt.bfloat16
    ALU, ACT, AX = mybir.AluOpType, mybir.ActivationFunctionType, mybir.AxisListType

    y_dram = [nc.dram_tensor(f"y_dir{d}", [NCH, P, CT * T], fp32, kind="Internal").ap() for d in (0, 1)]
    z_dram = nc.dram_tensor("silu_z", [NCH, P, CT * T], fp32, kind="Internal").ap()
    x_chunk = x.rearrange("(c t p) e -> c p t e", t=TT, p=P)
    out_chunk = out.rearrange("(c t p) e -> c p t e", t=TT, p=P)

    ctx = ExitStack()
    with ctx:
        def sem(name):
            return ctx.enter_context(nc.semaphore(name))

        with ExitStack() as one:
            def sb(name, shape, dt=fp32):
                return one.enter_context(nc.sbuf_tensor(name, shape, dt))

            def pb(name, shape):
                return one.enter_context(nc.psum_tensor(name, shape, fp32))

            ident = sb("ident", [P, P])
            w_in = sb("w_in", [P, KC, 2 * DI])
            w_x = sb("w_x", [P, 2, CT, P])
            w_dt = sb("w_dt", [RANK, 2, DI])
            taps = sb("taps", [P, 2, CT, TAPS])
            tap_diag = sb("tap_diag", [P, 2, CT, TAPS, P])
            skip = sb("skip", [P, 2, CT])
            skip_diag = sb("skip_diag", [P, 2, CT, P])
            b_conv = sb("b_conv", [P, 2, CT])
            b_dt = sb("b_dt", [P, 2, CT])
            w_norm = sb("w_norm", [P, KC])
            neg_a = sb("neg_a", [P, 2, CT, NS])
            row_sel = sb("row_sel", [P, 32], bf16)
            limits = sb("limits", [P, 2, NCH + 1])
            limit_now = sb("limit_now", [P, 2, 2])
            half_power = sb("half_power", [P, TT])
            xb = sb("xb", [P, TT, DM])
            junk = sb("junk", [P, TT, DM])
            sq = sb("sq", [P, TT])
            rstd = sb("rstd", [P, TT])
            xnT = sb("xnT", [P, KC, T])
            xi = sb("xi", [P, 2, CT, T + HALO])
            xc = sb("xc", [P, CT, T])
            sz = sb("sz", [P, CT, T])
            parts = sb("parts", [P, 2, T], bf16)
            part_f = sb("part_f", [P, T])
            part_m = sb("part_m", [P, T], bf16)
            dt_in = sb("dt_in", [RANK, T])
            ebuf = sb("ebuf", [P, CT, T])
            series = sb("series", [P, CT, T])
            series_b = sb("series_b", [P, 1])
            delta = sb("delta", [P, 2, CT, T])
            dx = sb("dx", [P, 2, CT, T])
            decay = sb("decay", [P, 2, CT, SEG])
            state = sb("state", [P, RING, CT, SEG])
            c_sb = sb("c_sb", [P, 2, T])
            carry = sb("carry", [P, 2, NS, CT])
            ys = sb("ys", [P, CT, T])

            y_ps = pb("y_ps", [P, CT, T])
            b_ps = pb("b_ps", [P, T])
            c_ps = pb("c_ps", [P, T])
            work = [pb(f"work{k}", [P, T]) for k in (0, 1)]

            spare = sem("spare")
            s_small = sem("s_small")
            s_xproj = sem("s_xproj")
            s_ident = sem("s_ident")
            s_sel = sem("s_sel")
            s_zeroed = sem("s_zeroed")
            s_diags = sem("s_diags")
            s_aexp = sem("s_aexp")
            s_nega = sem("s_nega")
            s_xpad = sem("s_xpad")
            x_loaded = sem("x_loaded")
            sq_done = sem("sq_done")
            rstd_mid = sem("rstd_mid")
            rstd_done = sem("rstd_done")
            xn_done = sem("xn_done")
            xT_ready = sem("xT_ready")
            xT_taken = sem("xT_taken")
            xi_ready = sem("xi_ready")
            xi_taken = sem("xi_taken")
            conv_ready = sem("conv_ready")
            conv_taken = sem("conv_taken")
            halo_moved = sem("halo_moved")
            z_ready = sem("z_ready")
            z_taken = sem("z_taken")
            silu_done = sem("silu_done")
            sz_ready = sem("sz_ready")
            sz_stored = sem("sz_stored")
            xdbl_ready = sem("xdbl_ready")
            high_ready = sem("high_ready")
            dt_taken = sem("dt_taken")
            rest_ready = sem("rest_ready")
            mid_ready = sem("mid_ready")
            split_done = sem("split_done")
            pre_ready = sem("pre_ready")
            pre_taken = sem("pre_taken")
            e_ready = sem("e_ready")
            square_ready = sem("square_ready")
            series_ready = sem("series_ready")
            log_ready = sem("log_ready")
            soft_ready = sem("soft_ready")
            delta_ready = sem("delta_ready")
            dx_ready = sem("dx_ready")
            b_ready = sem("b_ready")
            c_ready = sem("c_ready")
            c_copied = sem("c_copied")
            decay_ready = sem("decay_ready")
            carry_in = sem("carry_in")
            drive_ready = sem("drive_ready")
            scan_done = sem("scan_done")
            carry_out = sem("carry_out")
            limit_set = sem("limit_set")
            hc_dve = sem("hc_dve")
            hc_pool = sem("hc_pool")
            skip_added = sem("skip_added")
            reduced = sem("reduced")
            y_taken = sem("y_taken")
            y_stored = sem("y_stored")

            SMALL = 13

            def last_column(d):
                return T if d == 0 else 1

            def carry_column(d):
                return 0 if d == 0 else SEG - 1

            def xdbl_slot(d):
                return 8 if d == 0 else 6

            def run(eng, unit):
                unit(0, 0, True)
                unit(0, 1, False)
                with eng.Fori(1, NCH) as i:
                    unit(i, 0, False)
                    unit(i, 1, False)

            block = one.enter_context(nc.Block())

            @block.sync
            def _(sp):
                sp.dma_start(w_norm[:, :], norm_w).then_inc(s_small, 16)
                sp.dma_start(w_in[:, :, :], in_w.rearrange("(k p) e -> p k e", p=P)).then_inc(s_small, 16)
                sp.dma_start(xb[:, :, :], x_chunk[0, :, :, :]).then_inc(x_loaded, 16)
                for d in (0, 1):
                    sp.dma_start(taps[:, d, :, :], conv_w[d]).then_inc(s_small, 16)
                    sp.dma_start(b_conv[:, d, :], conv_b[d]).then_inc(s_small, 16)
                    sp.dma_start(skip[:, d, :], d_skip[d]).then_inc(s_small, 16)
                    sp.dma_start(b_dt[:, d, :], dt_b[d]).then_inc(s_small, 16)
                    sp.dma_start(neg_a[:, d, :, :], a_log[d]).then_inc(s_small, 16)
                sp.dma_start(w_dt[:, :, :], dt_w.rearrange("d r e -> r d e")).then_inc(s_small, 16)
                sp.wait_ge(s_xpad, 1)
                for d in (0, 1):
                    w = xproj_w[d].rearrange("(t p) e -> p t e", p=P)
                    sp.dma_start(w_x[:, d, :, 0:RANK], w[:, :, 0:RANK]).then_inc(s_xproj, 16)
                    for q in (1, 2, 3):
                        sp.dma_start(w_x[:, d, :, 32 * q:32 * q + 32], w[:, :, RANK:RANK + 2 * NS]).then_inc(s_xproj, 16)

                sp.wait_ge(xT_ready, 2)
                sp.dma_start(xb[:, :, :], x_chunk[rank_of_backward(0), :, :, :]).then_inc(x_loaded, 16)

                def unit(i, d, first):
                    u = 2 * i + d
                    j = (i + 1) % NCH if isinstance(i, int) else (i + 1) & (NCH - 1)
                    hold(sp, xT_ready, 2 * (u + 1) + 2, spare)
                    sp.dma_start(xb[:, :, :], x_chunk[j if d == 0 else rank_of_backward(j), :, :, :]).then_inc(x_loaded, 16)
                    if not first:
                        hold(sp, y_taken, u, spare)
                        c = i if d == 1 else rank_of_backward(i - 1)
                        sp.dma_start(y_dram[1 - d][c, :, :], ys[:, :, :].rearrange("p t n -> p (t n)")).then_inc(y_stored, 16)
                    if d == 1:
                        hold(sp, sz_ready, i + 2, spare)
                        sp.dma_start(z_dram[j, :, :], sz[:, :, :].rearrange("p t n -> p (t n)")).then_inc(sz_stored, 16)

                sp.wait_ge(sz_ready, 1)
                sp.dma_start(z_dram[0, :, :], sz[:, :, :].rearrange("p t n -> p (t n)")).then_inc(sz_stored, 16)
                run(sp, unit)
                sp.wait_ge(y_taken, 2 * NCH)
                sp.dma_start(y_dram[1][rank_of_backward(NCH - 1), :, :], ys[:, :, :].rearrange("p t n -> p (t n)")).then_inc(y_stored, 16)
                sp.wait_ge(y_stored, 16 * 2 * NCH)
                sp.wait_ge(sz_stored, 16 * (NCH + 1))
                sp.wait_ge(x_loaded, 16 * (2 * NCH + 2))

            @block.tensor
            def _(pe):
                w = work

                def project(slot, p, d, j):
                    q = xdbl_slot(d)
                    if slot == 1:
                        pe.wait_ge(xn_done, p + 1)
                        wait(pe, pre_taken, 4 * p)
                        for k in range(KC):
                            for t in range(TT):
                                last = nc.tensor.transpose(w[k][:, t * P:(t + 1) * P], xb[:, t, k * P:(k + 1) * P], ident[:, :])
                            last.then_inc(xT_ready, 1)
                    if slot in (2, 3):
                        for m in (2 * slot - 4, 2 * slot - 3):
                            if m == 0:
                                pe.wait_ge(xT_taken, 2 * p + 2)
                            if m >= 2:
                                pe.wait_ge(xi_taken, 4 * p + m - 1)
                            for k in range(KC):
                                last = nc.tensor.matmul(w[m % 2][:, :], w_in[:, k, m * P:(m + 1) * P], xnT[:, k, :],
                                                        start=(k == 0), stop=(k == KC - 1))
                            last.then_inc(xi_ready, 1)
                    if slot in (4, 5):
                        for m in (2 * slot - 8, 2 * slot - 7):
                            if m == 0:
                                pe.wait_ge(xi_taken, 4 * p + 4)
                            if m >= 2:
                                pe.wait_ge(conv_taken, 4 * p + m - 1)
                            for k in range(TAPS):
                                at = k if d == 0 else HALO - k
                                last = nc.tensor.matmul(w[m % 2][:, :], tap_diag[:, d, m, k, :], xi[:, d, m, at:at + T],
                                                        start=(k == 0), stop=(k == TAPS - 1))
                            last.then_inc(conv_ready, 1)
                    if slot in (6, 7) and d == 0:
                        for m in (2 * slot - 12, 2 * slot - 11):
                            if m < 2:
                                pe.wait_ge(conv_taken, 4 * p + 3 + m)
                            else:
                                pe.wait_ge(z_taken, 4 * j + m - 1)
                            for k in range(KC):
                                last = nc.tensor.matmul(w[m % 2][:, :], w_in[:, k, DI + m * P:DI + (m + 1) * P], xnT[:, k, :],
                                                        start=(k == 0), stop=(k == KC - 1))
                            last.then_inc(z_ready, 1)
                    if slot == q:
                        pe.wait_ge(silu_done, p + 1)
                        if d == 0:
                            pe.wait_ge(z_taken, 4 * j + 4)
                        for m in range(CT):
                            last = nc.tensor.matmul(w[0][:, :], w_x[:, d, m, :], xc[:, m, :], start=(m == 0), stop=(m == CT - 1))
                        last.then_inc(xdbl_ready, 1)
                    if slot in (q + 1, q + 2):
                        for m in (2 * (slot - q) - 2, 2 * (slot - q) - 1):
                            if m == 0:
                                pe.wait_ge(dt_taken, p + 1)
                            if m == 1:
                                pe.wait_ge(rest_ready, p + 1)
                            if m >= 2:
                                pe.wait_ge(pre_taken, 4 * p + m - 1)
                            last = nc.tensor.matmul(w[(m + 1) % 2][:, :], w_dt[:, d, m * P:(m + 1) * P], dt_in[:, :], start=True, stop=True)
                            last.then_inc(pre_ready, 1)

                def reduce(u, m):
                    if m in ON_DVE:
                        pe.wait_ge(hc_dve, N_DVE * u + before(m, True) + 1)
                    else:
                        pe.wait_ge(hc_pool, N_POOL * u + before(m, False) + 1)
                    for t in range(CT):
                        last = nc.tensor.matmul(y_ps[:, t, :], ident[:, :], state[:, m % RING, t, 1:T + 1], start=False, stop=(m == NS - 1))
                    last.then_inc(reduced, 1)

                def unit(i, d, first):
                    u = 2 * i + d
                    for n in range(NS):
                        wait(pe, drive_ready, 16 * u + n)
                        if n == 0:
                            pe.wait_ge(split_done, u + 1)
                        nc.tensor.matmul(b_ps[:, :], row_sel[:, n:n + 1].to_broadcast([P, P]), parts[:, d, :],
                                         start=True, stop=True).then_inc(b_ready, 1)
                        if (n - 1) in ON_DVE:
                            pe.wait_ge(hc_dve, N_DVE * u + before(n, True))
                        else:
                            wait(pe, c_copied, N_POOL * u + before(n, False))
                        nc.tensor.matmul(c_ps[:, :], row_sel[:, NS + n:NS + n + 1].to_broadcast([P, P]), parts[:, d, :],
                                         start=True, stop=True).then_inc(c_ready, 1)
                        if n < LAG and not first:
                            reduce(u - 1, NS - LAG + n)
                        if n == LAG:
                            wait(pe, y_taken, u)
                            for t in range(CT):
                                last = nc.tensor.matmul(y_ps[:, t, :], skip_diag[:, d, t, :], xc[:, t, :], start=True, stop=False)
                            last.then_inc(skip_added, 1)
                        if n >= LAG:
                            reduce(u, n - LAG)
                        project(n, u + 1, 1 - d, i + d)

                pe.wait_ge(s_ident, 2)
                pe.wait_ge(s_small, 16 * SMALL)
                pe.wait_ge(s_diags, 1)
                pe.wait_ge(s_xproj, 16 * 8)
                pe.wait_ge(s_sel, 4)
                for slot in range(NS):
                    project(slot, 0, 0, 0)
                run(pe, unit)
                for m in range(NS - LAG, NS):
                    reduce(2 * NCH - 1, m)

            @block.scalar
            def _(act):
                def project(slot, p, d, j):
                    q = xdbl_slot(d)
                    if slot == 0:
                        act.wait_ge(x_loaded, 16 * (p + 1))
                        wait(act, xn_done, p)
                        for t in range(TT):
                            last = nc.scalar.activation(junk[:, t, :], xb[:, t, :], ACT.Square, accum_out=sq[:, t:t + 1])
                        last.then_inc(sq_done, 1)
                    if slot == 2:
                        for k in range(KC):
                            act.wait_ge(xT_ready, 2 * p + k + 1)
                            nc.scalar.activation(xnT[:, k, :], work[k][:, :], ACT.Copy, scale=w_norm[:, k:k + 1]).then_inc(xT_taken, 1)
                    if slot in (3, 4):
                        for m in (2 * slot - 6, 2 * slot - 5):
                            act.wait_ge(xi_ready, 4 * p + m + 1)
                            if m == 0:
                                wait(act, halo_moved, p - 1)
                            at = HALO if d == 0 else 0
                            nc.scalar.activation(xi[:, d, m, at:at + T], work[m % 2][:, :], ACT.Copy).then_inc(xi_taken, 1)
                    if slot in (5, 6):
                        for m in (2 * slot - 10, 2 * slot - 9):
                            act.wait_ge(conv_ready, 4 * p + m + 1)
                            if m == 0:
                                wait(act, skip_added, p)
                            nc.scalar.activation(xc[:, m, :], work[m % 2][:, :], ACT.Identity, bias=b_conv[:, d, m:m + 1]).then_inc(conv_taken, 1)
                    if slot in (7, 8) and d == 0:
                        for m in (2 * slot - 14, 2 * slot - 13):
                            act.wait_ge(z_ready, 4 * j + m + 1)
                            if m == 0:
                                wait(act, sz_stored, 16 * j)
                            nc.scalar.activation(sz[:, m, :], work[m % 2][:, :], ACT.Copy).then_inc(z_taken, 1)
                    if slot == q:
                        act.wait_ge(conv_taken, 4 * p + 4)
                        nc.scalar.activation(xc[:, :, :], xc[:, :, :], ACT.Silu).then_inc(silu_done, 1)
                        if d == 0:
                            act.wait_ge(z_taken, 4 * j + 4)
                            nc.scalar.activation(sz[:, :, :], sz[:, :, :], ACT.Silu).then_inc(sz_ready, 1)
                    if slot == q + 1:
                        act.wait_ge(xdbl_ready, p + 1)
                        nc.scalar.activation(parts[:, d, :], work[0][:, :], ACT.Copy).then_inc(high_ready, 1)
                        nc.scalar.activation(dt_in[:, :], work[0][0:RANK, :], ACT.Copy).then_inc(dt_taken, 1)
                    if slot in (q + 2, q + 3):
                        for m in (2 * (slot - q) - 4, 2 * (slot - q) - 3):
                            act.wait_ge(pre_ready, 4 * p + m + 1)
                            if m == 0:
                                wait(act, delta_ready, p)
                            nc.scalar.activation(ebuf[:, m, :], work[(m + 1) % 2][:, :], ACT.Abs, bias=b_dt[:, d, m:m + 1])
                            nc.scalar.activation(delta[:, d, m, :], work[(m + 1) % 2][:, :], ACT.Relu, bias=b_dt[:, d, m:m + 1]).then_inc(pre_taken, 1)
                    if slot == q + 3:
                        act.wait_ge(pre_taken, 4 * p + 4)
                        nc.scalar.activation(ebuf[:, :, :], ebuf[:, :, :], ACT.Exp, scale=-1.0).then_inc(e_ready, 1)
                        act.wait_ge(e_ready, p + 1)
                        nc.scalar.activation(series[:, :, :], ebuf[:, :, :], ACT.Square, scale=SERIES_A, bias=series_b[:, 0:1]).then_inc(square_ready, 1)
                    if slot == q + 5:
                        act.wait_ge(series_ready, p + 1)
                        nc.scalar.activation(ebuf[:, :, :], ebuf[:, :, :], ACT.Ln, bias=1.0).then_inc(log_ready, 1)

                def unit(i, d, first):
                    u = 2 * i + d
                    for n in range(NS):
                        if n == 0:
                            act.wait_ge(delta_ready, u + 1)
                        wait(act, scan_done, 16 * u + n - 1)
                        for t in range(CT):
                            last = nc.scalar.activation(decay[:, n % 2, t, 1:T + 1], delta[:, d, t, :], ACT.Exp, scale=neg_a[:, d, t, n:n + 1])
                        last.then_inc(decay_ready, 1)
                        if not (isinstance(i, int) and i == 0):
                            act.wait_ge(carry_out, 16 * u + n - 31)
                        if not (first and n < RING):
                            act.wait_ge(reduced, 16 * u + n - RING + 1)
                        nc.scalar.activation(state[:, n % RING, :, carry_column(d)], carry[:, d, n, :], ACT.Copy).then_inc(carry_in, 1)
                        if n == LAG and not first:
                            act.wait_ge(reduced, 16 * u)
                            wait(act, y_stored, 16 * (u - 1))
                            nc.scalar.activation(ys[:, :, :], y_ps[:, :, :], ACT.Copy).then_inc(y_taken, 1)
                        if n not in ON_DVE:
                            c = N_POOL * u + before(n, False)
                            act.wait_ge(c_ready, 16 * u + n + 1)
                            if not (first and before(n, False) < 2):
                                act.wait_ge(hc_pool, c - 1)
                            nc.scalar.activation(c_sb[:, before(n, False) % 2, :], c_ps[:, :], ACT.Copy).then_inc(c_copied, 1)
                        project(n, u + 1, 1 - d, i + d)

                act.wait_ge(s_small, 16 * SMALL)
                nc.scalar.activation(neg_a[:, :, :, :], neg_a[:, :, :, :], ACT.Exp).then_inc(s_aexp, 1)
                act.wait_ge(s_nega, 1)
                act.wait_ge(s_zeroed, 6)
                for slot in range(NS):
                    project(slot, 0, 0, 0)
                run(act, unit)
                act.wait_ge(reduced, 16 * 2 * NCH)
                act.wait_ge(y_stored, 16 * (2 * NCH - 1))
                nc.scalar.activation(ys[:, :, :], y_ps[:, :, :], ACT.Copy).then_inc(y_taken, 1)

            @block.vector
            def _(dve):
                def project(slot, p, d, j):
                    q = xdbl_slot(d)
                    if slot == 0:
                        dve.wait_ge(rstd_done, p + 1)
                        for t in range(TT):
                            last = nc.vector.tensor_scalar(xb[:, t, :], xb[:, t, :], rstd[:, t:t + 1], None, ALU.mult)
                        last.then_inc(xn_done, 1)
                    if slot == 6:
                        dve.wait_ge(conv_ready, 4 * p + 4)
                        src, dst = (T, 0) if d == 0 else (0, T)
                        nc.vector.tensor_scalar(xi[:, d, :, dst:dst + HALO], xi[:, d, :, src:src + HALO],
                                                limits[:, 0, bass.ds(j, 1)], limits[:, 1, bass.ds(j, 1)], ALU.min, ALU.max).then_inc(halo_moved, 1)
                    if slot == q + 1:
                        dve.wait_ge(high_ready, p + 1)
                        nc.vector.tensor_tensor(out=part_f[64:128, :], in0=work[0][64:128, :], in1=parts[64:128, d, :], op=ALU.subtract).then_inc(rest_ready, 1)
                        dve.wait_ge(rest_ready, p + 1)
                        nc.vector.tensor_copy(parts[64:96, d, :], part_f[64:96, :])
                        nc.vector.tensor_copy(part_m[96:128, :], part_f[96:128, :]).then_inc(mid_ready, 1)
                        dve.wait_ge(mid_ready, p + 1)
                        nc.vector.tensor_tensor(out=parts[96:128, d, :], in0=part_f[96:128, :], in1=part_m[96:128, :], op=ALU.subtract).then_inc(split_done, 1)
                    if slot == q + 4:
                        dve.wait_ge(square_ready, p + 1)
                        nc.vector.scalar_tensor_tensor(out=series[:, :, :], in0=series[:, :, :], scalar=SERIES_C, in1=ebuf[:, :, :],
                                                       op0=ALU.add, op1=ALU.mult).then_inc(series_ready, 1)
                    if slot == q + 5:
                        dve.wait_ge(log_ready, p + 1)
                        nc.vector.scalar_tensor_tensor(out=ebuf[:, :, :], in0=ebuf[:, :, :], scalar=LOG_MARGIN, in1=series[:, :, :],
                                                       op0=ALU.add, op1=ALU.min).then_inc(soft_ready, 1)

                def unit(i, d, first):
                    u = 2 * i + d
                    for n in range(NS):
                        if n == 0:
                            dve.wait_ge(dx_ready, u + 1)
                        dve.wait_ge(b_ready, 16 * u + n + 1)
                        if not (first and n < RING):
                            dve.wait_ge(reduced, 16 * u + n - RING + 1)
                        nc.vector.tensor_tensor(out=state[:, n % RING, :, 1:T + 1], in0=dx[:, d, :, :],
                                                in1=b_ps[:, :].unsqueeze(1).to_broadcast([P, CT, T]), op=ALU.mult).then_inc(drive_ready, 1)
                        dve.wait_ge(drive_ready, 16 * u + n + 1)
                        dve.wait_ge(decay_ready, 16 * u + n + 1)
                        dve.wait_ge(carry_in, 16 * u + n + 1)
                        step = slice(None, None, 1 if d == 0 else -1)
                        a = decay[:, n % 2, :, :].rearrange("p t n -> p (t n)")[:, step]
                        b = state[:, n % RING, :, :].rearrange("p t n -> p (t n)")[:, step]
                        nc.vector.tensor_tensor_scan(b, a, b, 0.0, ALU.mult, ALU.add).then_inc(scan_done, 1)
                        if n in ON_DVE:
                            dve.wait_ge(scan_done, 16 * u + n + 1)
                            dve.wait_ge(c_ready, 16 * u + n + 1)
                            dve.wait_ge(carry_out, 16 * u + n + 1)
                            nc.vector.tensor_tensor(out=state[:, n % RING, :, 1:T + 1], in0=state[:, n % RING, :, 1:T + 1],
                                                    in1=c_ps[:, :].unsqueeze(1).to_broadcast([P, CT, T]), op=ALU.mult).then_inc(hc_dve, 1)
                        if n == 4:
                            dve.wait_ge(carry_out, 16 * u + 1)
                            nc.vector.tensor_copy(limit_now[:, 1 - d, :], limits[:, :, bass.ds(i + d, 1)].rearrange("p a o -> p (a o)")).then_inc(limit_set, 1)
                        project(n, u + 1, 1 - d, i + d)

                dve.wait_ge(s_ident, 2)
                dve.wait_ge(s_small, 16 * SMALL)
                for d in (0, 1):
                    for t in range(CT):
                        for k in range(TAPS):
                            nc.vector.tensor_scalar(tap_diag[:, d, t, k, :], ident[:, :], taps[:, d, t, k:k + 1], None, ALU.mult)
                        last = nc.vector.tensor_scalar(skip_diag[:, d, t, :], ident[:, :], skip[:, d, t:t + 1], None, ALU.mult)
                last.then_inc(s_diags, 1)
                dve.wait_ge(s_aexp, 1)
                nc.vector.tensor_scalar(neg_a[:, :, :, :], neg_a[:, :, :, :], -1.0, None, ALU.mult).then_inc(s_nega, 1)
                dve.wait_ge(s_zeroed, 6)
                nc.vector.tensor_copy(limit_now[:, 0, :], limits[:, :, 0]).then_inc(limit_set, 1)
                for slot in range(NS):
                    project(slot, 0, 0, 0)
                run(dve, unit)

            @block.gpsimd
            def _(pool):
                def project(slot, p, d, j):
                    q = xdbl_slot(d)
                    if slot == 0:
                        hold(pool, sq_done, p + 1, spare)
                        nc.gpsimd.tensor_scalar(rstd[:, :], sq[:, :], 1.0 / DM, EPS, ALU.mult, ALU.add).then_inc(rstd_mid, 1)
                        pool.wait_ge(rstd_mid, p + 1)
                        nc.gpsimd.tensor_tensor(out=rstd[:, :], in0=rstd[:, :], in1=half_power[:, :], op=ALU.pow).then_inc(rstd_done, 1)
                    if slot == q + 5:
                        pool.wait_ge(soft_ready, p + 1)
                        nc.gpsimd.tensor_tensor(out=delta[:, d, :, :], in0=delta[:, d, :, :], in1=ebuf[:, :, :], op=ALU.add).then_inc(delta_ready, 1)
                    if slot == q + 6:
                        pool.wait_ge(delta_ready, p + 1)
                        nc.gpsimd.tensor_tensor(out=dx[:, d, :, :], in0=delta[:, d, :, :], in1=xc[:, :, :], op=ALU.mult).then_inc(dx_ready, 1)

                def unit(i, d, first):
                    u = 2 * i + d
                    pool.wait_ge(limit_set, u + 1)
                    for n in range(NS):
                        hold(pool, scan_done, 16 * u + n + 1, spare)
                        nc.gpsimd.tensor_scalar(carry[:, d, n, :], state[:, n % RING, :, last_column(d)],
                                                limit_now[:, d, 0:1], limit_now[:, d, 1:2], ALU.min, ALU.max).then_inc(carry_out, 1)
                        if n not in ON_DVE:
                            c = N_POOL * u + before(n, False)
                            pool.wait_ge(c_copied, c + 1)
                            pool.wait_ge(carry_out, 16 * u + n + 1)
                            nc.gpsimd.tensor_tensor(out=state[:, n % RING, :, 1:T + 1], in0=state[:, n % RING, :, 1:T + 1],
                                                    in1=c_sb[:, before(n, False) % 2, :].unsqueeze(1).to_broadcast([P, CT, T]), op=ALU.mult).then_inc(hc_pool, 1)
                        project(n, u + 1, 1 - d, i + d)

                nc.gpsimd.memset(w_x[:, :, :, :], 0.0).then_inc(s_xpad, 1)
                nc.gpsimd.memset(ident[:, :], 0.0).then_inc(s_ident, 1)
                nc.gpsimd.memset(row_sel[:, :], 0.0).then_inc(s_sel, 1)
                nc.gpsimd.memset(decay[:, :, :, :], 0.0).then_inc(s_zeroed, 1)
                nc.gpsimd.memset(state[:, :, :, :], 0.0).then_inc(s_zeroed, 1)
                nc.gpsimd.memset(xi[:, :, :, :], 0.0).then_inc(s_zeroed, 1)
                nc.gpsimd.memset(carry[:, :, :, :], 0.0).then_inc(s_zeroed, 1)
                nc.gpsimd.memset(half_power[:, :], -0.5)
                nc.gpsimd.memset(series_b[:, :], SERIES_B)
                nc.gpsimd.memset(limits[:, 0, :], HUGE)
                nc.gpsimd.memset(limits[:, 1, :], -HUGE).then_inc(s_zeroed, 1)
                pool.wait_ge(s_zeroed, 5)
                nc.gpsimd.memset(limits[:, :, CPB - 1:NCH:CPB], 0.0).then_inc(s_zeroed, 1)
                pool.wait_ge(s_ident, 1)
                nc.gpsimd.affine_select(out=ident[:, :], in_=ident[:, :], compare_op=ALU.not_equal, fill=1.0,
                                        base=0, pattern=[[-1, P]], channel_multiplier=1).then_inc(s_ident, 1)
                for q in (1, 2, 3):
                    pool.wait_ge(s_sel, q)
                    nc.gpsimd.affine_select(out=row_sel[:, :], in_=row_sel[:, :], compare_op=ALU.not_equal, fill=1.0,
                                            base=-32 * q, pattern=[[-1, 32]], channel_multiplier=1).then_inc(s_sel, 1)
                for slot in range(NS):
                    project(slot, 0, 0, 0)
                run(pool, unit)

        experts(nc, sem, x_chunk, out_chunk, y_dram, z_dram, out_w, gate_w, gate_b, expert_w, expert_b)


def experts(nc, sem, x_chunk, out_chunk, y_dram, z_dram, out_w, gate_w, gate_b, expert_w, expert_b):
    fp32 = mybir.dt.float32
    ALU, ACT, AX = mybir.AluOpType, mybir.ActivationFunctionType, mybir.AxisListType
    EP = NE // 2
    with ExitStack() as two:
        def sb(name, shape, dt=fp32):
            return two.enter_context(nc.sbuf_tensor(name, shape, dt))

        def pb(name, shape):
            return two.enter_context(nc.psum_tensor(name, shape, fp32))

        ident = sb("ident2", [P, P])
        w_out = sb("w_out", [P, CT, DM])
        w_gate = sb("w_gate", [P, KC, NR])
        b_gate = sb("b_gate", [P, NR])
        w_exp = sb("w_exp", [P, KC, NE * DM])
        b_exp = sb("b_exp", [1, NE * DM])
        ones = sb("ones", [1, P])
        first_key = sb("first_key", [P, TT, NR])
        half_power = sb("half_power2", [P, TT])
        yf = sb("yf", [P, 2, CT, T])
        yb = sb("yb", [P, 2, CT, T])
        sz = sb("sz2", [P, 2, CT, T])
        xr = sb("xr", [P, 2, TT, DM])
        v = sb("v", [P, 2, TT, DM])
        x1T = sb("x1T", [P, KC, T])
        stats = sb("stats", [P, TT, 6])
        mv = sb("mv", [P, TT, 2])
        rs = sb("rs", [P, TT])
        lg = sb("lg", [P, TT, NR])
        pr = sb("pr", [P, TT, NR])
        left = sb("left", [P, TT, NR])
        key = sb("key", [P, TT, NR])
        hot1 = sb("hot1", [P, TT, NR])
        hot2 = sb("hot2", [P, TT, NR])
        red = sb("red", [P, 8, TT])
        cw = sb("cw", [P, TT, NR])

        pO = [pb(f"pO{k}", [P, T]) for k in (0, 1)]
        pT = [pb(f"pT{k}", [P, T]) for k in (0, 1)]
        pG = pb("pG", [P, T])
        pE = [pb(f"pE{k}", [P, T]) for k in (0, 1, 2)]

        spare2 = sem("spare2")
        w_loaded = sem("w2_loaded")
        made = sem("made2")
        in_loaded = [sem(f"in2_loaded{k}") for k in (0, 1)]
        gated = sem("gated")
        summed = sem("summed")
        proj_ready = sem("proj_ready")
        v_ready = sem("v_ready")
        stat_ready = sem("stat_ready")
        mv_ready = sem("mv_ready")
        rs_mid = sem("rs_mid")
        rs_ready = sem("rs_ready")
        x1_ready = sem("x1_ready")
        x1T_ready = sem("x1T_ready")
        x1T_taken = sem("x1T_taken")
        gate_ready = sem("gate_ready")
        lg_ready = sem("lg_ready")
        pr_ready = sem("pr_ready")
        chain = sem("chain2")
        exp_ready = sem("exp_ready")
        exp_taken = sem("exp_taken")
        stored = sem("stored")

        block = two.enter_context(nc.Block())

        @block.sync
        def _(sp):
            sp.dma_start(w_out[:, :, :], out_w.rearrange("(k p) e -> p k e", p=P)).then_inc(w_loaded, 16)
            sp.dma_start(w_gate[:, :, :], gate_w.rearrange("(k p) e -> p k e", p=P)).then_inc(w_loaded, 16)
            sp.dma_start(b_gate[:, :], gate_b.partition_broadcast(P)).then_inc(w_loaded, 16)
            sp.dma_start(b_exp[:, :], expert_b).then_inc(w_loaded, 16)
            for e in range(NE):
                sp.dma_start(w_exp[:, :, e * DM:(e + 1) * DM], expert_w[e].rearrange("(k p) e -> p k e", p=P)).then_inc(w_loaded, 16)

            def load(c, s):
                for dst, src in ((yf, y_dram[0]), (yb, y_dram[1]), (sz, z_dram)):
                    sp.dma_start(dst[:, s, :, :].rearrange("p t n -> p (t n)"), src[c, :, :]).then_inc(in_loaded[s], 16)
                sp.dma_start(xr[:, s, :, :], x_chunk[c, :, :, :]).then_inc(in_loaded[s], 16)

            load(0, 0)
            load(1, 1)

            def chunk(c, s, more):
                hold(sp, x1_ready, 2 * (c + 1), spare2)
                sp.dma_start(out_chunk[c, :, :, :], v[:, s, :, :]).then_inc(stored, 16)
                if more:
                    hold(sp, stored, 16 * (c + 1), spare2)
                    load(c + 2, s)

            with sp.Fori(0, NCH // 2 - 1) as g:
                for s in (0, 1):
                    chunk(2 * g + s, s, True)
            for s in (0, 1):
                chunk(NCH - 2 + s, s, False)
            sp.wait_ge(stored, 16 * NCH)

        @block.gpsimd
        def _(pool):
            nc.gpsimd.memset(ident[:, :], 0.0).then_inc(made, 1)
            nc.gpsimd.memset(half_power[:, :], -0.5)
            nc.gpsimd.memset(ones[:, :], 1.0)
            for e in range(NR):
                nc.gpsimd.memset(first_key[:, :, e], 16.0 - e)
            pool.wait_ge(made, 1)
            nc.gpsimd.affine_select(out=ident[:, :], in_=ident[:, :], compare_op=ALU.not_equal, fill=1.0,
                                    base=0, pattern=[[-1, P]], channel_multiplier=1).then_inc(made, 1)

            def root(k, c, eps):
                hold(pool, mv_ready, 2 * c + k + 1, spare2)
                nc.gpsimd.tensor_scalar(rs[:, :], mv[:, :, 1], eps, None, ALU.add).then_inc(rs_mid, 1)
                pool.wait_ge(rs_mid, 2 * c + k + 1)
                nc.gpsimd.tensor_tensor(out=rs[:, :], in0=rs[:, :], in1=half_power[:, :], op=ALU.pow).then_inc(rs_ready, 1)

            with pool.Fori(0, NCH // 2) as g:
                for s in (0, 1):
                    c = 2 * g + s
                    pool.wait_ge(summed, c + 1)
                    nc.gpsimd.tensor_tensor(out=yf[:, s, :, :], in0=yf[:, s, :, :], in1=sz[:, s, :, :], op=ALU.mult).then_inc(gated, 1)
                    root(0, c, 4 * EPS)
                    root(1, c, EPS)

        @block.tensor
        def _(pe):
            pe.wait_ge(w_loaded, 16 * (4 + NE))
            pe.wait_ge(made, 2)

            def chunk(c, s):
                pe.wait_ge(gated, c + 1)
                for t in range(TT):
                    for k in range(CT):
                        last = nc.tensor.matmul(pO[t // 2][:, (t % 2) * DM:(t % 2 + 1) * DM], yf[:, s, k, t * P:(t + 1) * P], w_out[:, k, :],
                                                start=(k == 0), stop=(k == CT - 1))
                    if t % 2:
                        last.then_inc(proj_ready, 1)
                pe.wait_ge(x1_ready, 2 * c + 1)
                for k in range(KC):
                    for t in range(TT):
                        last = nc.tensor.transpose(pT[k][:, t * P:(t + 1) * P], v[:, s, t, k * P:(k + 1) * P], ident[:, :])
                    last.then_inc(x1T_ready, 1)
                pe.wait_ge(x1T_taken, 2 * c + 2)
                for t in range(TT):
                    for k in range(KC):
                        last = nc.tensor.matmul(pG[:, t * NR:(t + 1) * NR], x1T[:, k, t * P:(t + 1) * P], w_gate[:, k, :],
                                                start=(k == 0), stop=(k == KC - 1))
                last.then_inc(gate_ready, 1)
                for t in range(TT):
                    for e in range(EP):
                        m = t * EP + e
                        pe.wait_ge(exp_taken, 32 * c + 2 * (m - 2)) if m >= 3 else None
                        cols = slice(e * 2 * DM, (e + 1) * 2 * DM)
                        for k in range(KC):
                            nc.tensor.matmul(pE[m % 3][:, :], x1T[:, k, t * P:(t + 1) * P], w_exp[:, k, cols], start=(k == 0), stop=False)
                        nc.tensor.matmul(pE[m % 3][:, :], ones[0:1, :], b_exp[0:1, cols], start=False, stop=True).then_inc(exp_ready, 1)

            with pe.Fori(0, NCH // 2) as g:
                for s in (0, 1):
                    chunk(2 * g + s, s)

        @block.scalar
        def _(act):
            with act.Fori(0, NCH // 2) as g:
                for s in (0, 1):
                    c = 2 * g + s
                    for k in range(KC):
                        act.wait_ge(x1T_ready, 2 * c + k + 1)
                        nc.scalar.activation(x1T[:, k, :], pT[k][:, :], ACT.Copy).then_inc(x1T_taken, 1)
                    act.wait_ge(lg_ready, c + 1)
                    nc.scalar.activation(pr[:, :, :], lg[:, :, :], ACT.Exp).then_inc(pr_ready, 1)

        @block.vector
        def _(dve):
            dve.wait_ge(made, 2)
            dve.wait_ge(w_loaded, 16 * (4 + NE))
            STEPS = 23

            def norm(k, c, s):
                for t in range(TT):
                    last = nc.vector.bn_stats(stats[:, t, :], v[:, s, t, :])
                last.then_inc(stat_ready, 1)
                hold(dve, stat_ready, 2 * c + k + 1, spare2)
                for t in range(TT):
                    last = nc.vector.bn_aggr(mv[:, t, :], stats[:, t, :])
                last.then_inc(mv_ready, 1)
                dve.wait_ge(rs_ready, 2 * c + k + 1)
                for t in range(TT):
                    last = nc.vector.tensor_scalar(v[:, s, t, :], v[:, s, t, :], mv[:, t, 0:1], rs[:, t:t + 1], ALU.subtract, ALU.mult)
                last.then_inc(x1_ready, 1)

            def chunk(g, s):
                c = 2 * g + s
                n = [0]

                def link(ins):
                    n[0] += 1
                    ins.then_inc(chain, 1)
                    dve.wait_ge(chain, STEPS * c + n[0])

                def over(col):
                    return red[:, col, :].unsqueeze(2).to_broadcast([P, TT, NR])

                dve.wait_ge(in_loaded[s], 64 * (g + 1))
                nc.vector.tensor_tensor(out=yf[:, s, :, :], in0=yf[:, s, :, :], in1=yb[:, s, :, :], op=ALU.add).then_inc(summed, 1)
                for k in (0, 1):
                    dve.wait_ge(proj_ready, 2 * c + k + 1)
                    nc.vector.scalar_tensor_tensor(out=v[:, s, 2 * k:2 * k + 2, :], in0=xr[:, s, 2 * k:2 * k + 2, :], scalar=4.0,
                                                   in1=pO[k][:, :].rearrange("p (t e) -> p t e", e=DM), op0=ALU.mult, op1=ALU.add).then_inc(v_ready, 1)
                dve.wait_ge(v_ready, 2 * c + 2)
                norm(0, c, s)
                dve.wait_ge(gate_ready, c + 1)
                link(nc.vector.tensor_tensor(out=lg[:, :, :], in0=pG[:, 0:TT * NR].rearrange("p (t e) -> p t e", e=NR),
                                             in1=b_gate[:, :].unsqueeze(1).to_broadcast([P, TT, NR]), op=ALU.add))
                link(nc.vector.tensor_reduce(red[:, 0, :], lg[:, :, :], AX.X, ALU.max))
                nc.vector.tensor_tensor(out=lg[:, :, :], in0=lg[:, :, :], in1=over(0), op=ALU.subtract).then_inc(lg_ready, 1)
                dve.wait_ge(pr_ready, c + 1)
                link(nc.vector.tensor_reduce(red[:, 1, :], pr[:, :, :], AX.X, ALU.add))
                link(nc.vector.reciprocal(red[:, 1, :], red[:, 1, :]))
                link(nc.vector.tensor_tensor(out=pr[:, :, :], in0=pr[:, :, :], in1=over(1), op=ALU.mult))
                for r, (src, hot) in enumerate(((pr, hot1), (left, hot2))):
                    link(nc.vector.tensor_reduce(red[:, 2, :], src[:, :, :], AX.X, ALU.max))
                    link(nc.vector.tensor_tensor(out=key[:, :, :], in0=src[:, :, :], in1=over(2), op=ALU.is_equal))
                    link(nc.vector.tensor_tensor(out=key[:, :, :], in0=key[:, :, :], in1=first_key[:, :, :], op=ALU.mult))
                    link(nc.vector.tensor_reduce(red[:, 3, :], key[:, :, :], AX.X, ALU.max))
                    link(nc.vector.tensor_tensor(out=hot[:, :, :], in0=key[:, :, :], in1=over(3), op=ALU.is_equal))
                    if r == 0:
                        link(nc.vector.scalar_tensor_tensor(out=left[:, :, :], in0=hot1[:, :, :], scalar=-2.0, in1=pr[:, :, :], op0=ALU.mult, op1=ALU.add))
                link(nc.vector.tensor_tensor(out=hot1[:, :, :], in0=hot1[:, :, :], in1=hot2[:, :, :], op=ALU.add))
                link(nc.vector.tensor_tensor(out=cw[:, :, :], in0=pr[:, :, :], in1=hot1[:, :, :], op=ALU.mult))
                link(nc.vector.tensor_reduce(red[:, 4, :], cw[:, :, 0:NE], AX.X, ALU.add))
                link(nc.vector.tensor_scalar(red[:, 5, :], red[:, 4, :], 0.0, None, ALU.is_le))
                link(nc.vector.tensor_tensor(out=red[:, 4, :], in0=red[:, 4, :], in1=red[:, 5, :], op=ALU.add))
                link(nc.vector.reciprocal(red[:, 4, :], red[:, 4, :]))
                link(nc.vector.tensor_tensor(out=cw[:, :, :], in0=cw[:, :, :], in1=over(4), op=ALU.mult))
                assert n[0] == STEPS
                for t in range(TT):
                    for e in range(NE):
                        m = t * EP + e // 2
                        dve.wait_ge(exp_ready, TT * EP * c + m + 1)
                        if e:
                            dve.wait_ge(exp_taken, 32 * c + t * NE + e)
                        nc.vector.scalar_tensor_tensor(out=v[:, s, t, :], in0=pE[m % 3][:, (e % 2) * DM:(e % 2 + 1) * DM],
                                                       scalar=cw[:, t, e:e + 1], in1=v[:, s, t, :], op0=ALU.mult, op1=ALU.add).then_inc(exp_taken, 1)
                dve.wait_ge(exp_taken, 32 * (c + 1))
                norm(1, c, s)

            with dve.Fori(0, NCH // 2) as g:
                for s in (0, 1):
                    chunk(g, s)


def kernel(**inputs):
    import numpy as np
    import concourse.bacc as bacc
    from concourse.bass_utils import run_bass_kernel_spmd as launch

    def channels(w):
        return np.ascontiguousarray(np.swapaxes(w.reshape((-1, P) + w.shape[1:]), 0, 1))

    a = {k.replace("L0_attn_", "").replace("L0_ffn_", ""): np.asarray(v) for k, v in inputs.items()}
    both = lambda name, f: np.stack([f(a[name + "_f"]), f(a[name + "_b"])])
    arrays = {
        "x": np.ascontiguousarray(a["x"].reshape(B * L, DM)),
        "in_w": np.ascontiguousarray(a["in_proj_w"].T),
        "out_w": np.ascontiguousarray(a["out_proj_w"].T),
        "norm_w": channels(a["norm_w"]),
        "conv_w": both("conv_w", lambda w: channels(w[:, 0, :])),
        "conv_b": both("conv_b", channels),
        "xproj_w": both("xproj_w", lambda w: np.ascontiguousarray(w.T)),
        "dt_w": both("dtproj_w", lambda w: np.ascontiguousarray(w.T)),
        "dt_b": both("dtproj_b", channels),
        "a_log": both("A_log", channels),
        "d_skip": both("D", channels),
        "gate_w": np.ascontiguousarray(a["gate_w"].T),
        "gate_b": a["gate_b"],
        "expert_w": a["expert_w"],
        "expert_b": np.ascontiguousarray(a["expert_b"].reshape(1, NE * DM)),
    }
    nc = bacc.Bacc("TRN2", target_bir_lowering=False, num_devices=1)
    aps = {k: nc.dram_tensor(f"in_{k}", v.shape, mybir.dt.from_np(v.dtype), kind="ExternalInput").ap() for k, v in arrays.items()}
    out = nc.dram_tensor("out", (B * L, DM), mybir.dt.float32, kind="ExternalOutput").ap()
    mamba_moe(nc, out=out, **aps)
    r = launch(nc, [{f"in_{k}": v for k, v in arrays.items()}], core_ids=[0])
    return r.results[0]["out"].reshape(B, L, DM)
```

```python
import concourse.bass as bass
from concourse import mybir
from contextlib import ExitStack

B, L, DM = 4, 2048, 256
DI, NS, TAPS, RANK = 512, 16, 4, 16
P = 128
T = 512
NCH = B * L // T
CPB = L // T
CT = DI // P
TT = T // P
KC = DM // P
HALO = TAPS - 1
SEG = T + 2
NE, NR = 8, 10
EPS = 1e-5
HUGE = 3.0e38
SERIES_A, SERIES_B, SERIES_C = 3 ** -0.5, -(3 ** 0.5) / 4, 13 / 16
LOG_MARGIN = 8e-8
ON_DVE = (12, 14)
RING = 4
XDBL = 8
LAG = 3
N_DVE, N_POOL = len(ON_DVE), NS - len(ON_DVE)


def before(n, on_dve):
    return sum((m in ON_DVE) == on_dve for m in range(n))


def wait(eng, sem, value):
    if not isinstance(value, int) or value > 0:
        eng.wait_ge(sem, value)


def hold(eng, sem, value, spare):
    eng.wait_ge(sem, value)
    eng.sem_inc(spare, 1)


def rank_of_backward(i):
    return (i & (NCH - CPB)) + (CPB - 1 - (i & (CPB - 1)))


def mamba_moe(nc, x, in_w, out_w, norm_w, conv_w, conv_b, xproj_w, dt_w, dt_b, a_log, d_skip,
              gate_w, gate_b, expert_w, expert_b, out):
    fp32, bf16 = mybir.dt.float32, mybir.dt.bfloat16
    ALU, ACT, AX = mybir.AluOpType, mybir.ActivationFunctionType, mybir.AxisListType

    y_dram = [nc.dram_tensor(f"y_dir{d}", [NCH, P, CT * T], fp32, kind="Internal").ap() for d in (0, 1)]
    z_dram = nc.dram_tensor("silu_z", [NCH, P, CT * T], fp32, kind="Internal").ap()
    x_chunk = x.rearrange("(c t p) e -> c p t e", t=TT, p=P)
    out_chunk = out.rearrange("(c t p) e -> c p t e", t=TT, p=P)

    ctx = ExitStack()
    with ctx:
        def sem(name):
            return ctx.enter_context(nc.semaphore(name))

        with ExitStack() as one:
            def sb(name, shape, dt=fp32):
                return one.enter_context(nc.sbuf_tensor(name, shape, dt))

            def pb(name, shape):
                return one.enter_context(nc.psum_tensor(name, shape, fp32))

            ident = sb("ident", [P, P])
            w_in = sb("w_in", [P, KC, 2 * DI])
            w_x = sb("w_x", [P, 2, CT, P])
            w_dt = sb("w_dt", [RANK, 2, DI])
            taps = sb("taps", [P, 2, CT, TAPS])
            tap_diag = sb("tap_diag", [P, 2, CT, TAPS, P])
            skip = sb("skip", [P, 2, CT])
            skip_diag = sb("skip_diag", [P, 2, CT, P])
            b_conv = sb("b_conv", [P, 2, CT])
            b_dt = sb("b_dt", [P, 2, CT])
            w_norm = sb("w_norm", [P, KC])
            neg_a = sb("neg_a", [P, 2, CT, NS])
            row_sel = sb("row_sel", [P, 32], bf16)
            limits = sb("limits", [P, 2, NCH + 1])
            limit_now = sb("limit_now", [P, 2, 2])
            half_power = sb("half_power", [P, TT])
            xb = sb("xb", [P, TT, DM])
            junk = sb("junk", [P, TT, DM])
            sq = sb("sq", [P, TT])
            rstd = sb("rstd", [P, TT])
            xnT = sb("xnT", [P, KC, T])
            xi = sb("xi", [P, 2, CT, T + HALO])
            xc = sb("xc", [P, CT, T])
            sz = sb("sz", [P, CT, T])
            parts = sb("parts", [P, 2, T], bf16)
            part_f = sb("part_f", [P, T])
            part_m = sb("part_m", [P, T], bf16)
            dt_in = sb("dt_in", [RANK, T])
            ebuf = sb("ebuf", [P, CT, T])
            series = sb("series", [P, CT, T])
            series_b = sb("series_b", [P, 1])
            delta = sb("delta", [P, 2, CT, T])
            dx = sb("dx", [P, 2, CT, T])
            decay = sb("decay", [P, 2, CT, SEG])
            state = sb("state", [P, RING, CT, SEG])
            c_sb = sb("c_sb", [P, 2, T])
            carry = sb("carry", [P, 2, NS, CT])
            ys = sb("ys", [P, CT, T])

            y_ps = pb("y_ps", [P, CT, T])
            b_ps = pb("b_ps", [P, T])
            c_ps = pb("c_ps", [P, T])
            work = [pb(f"work{k}", [P, T]) for k in (0, 1)]

            spare = sem("spare")
            s_small = sem("s_small")
            s_xproj = sem("s_xproj")
            s_ident = sem("s_ident")
            s_sel = sem("s_sel")
            s_zeroed = sem("s_zeroed")
            s_diags = sem("s_diags")
            s_aexp = sem("s_aexp")
            s_nega = sem("s_nega")
            s_xpad = sem("s_xpad")
            x_loaded = sem("x_loaded")
            sq_done = sem("sq_done")
            rstd_mid = sem("rstd_mid")
            rstd_done = sem("rstd_done")
            xn_done = sem("xn_done")
            xT_ready = sem("xT_ready")
            xT_taken = sem("xT_taken")
            xi_ready = sem("xi_ready")
            xi_taken = sem("xi_taken")
            conv_ready = sem("conv_ready")
            conv_taken = sem("conv_taken")
            halo_moved = sem("halo_moved")
            z_ready = sem("z_ready")
            z_taken = sem("z_taken")
            silu_done = sem("silu_done")
            sz_ready = sem("sz_ready")
            sz_stored = sem("sz_stored")
            xdbl_ready = sem("xdbl_ready")
            high_ready = sem("high_ready")
            dt_taken = sem("dt_taken")
            rest_ready = sem("rest_ready")
            mid_ready = sem("mid_ready")
            split_done = sem("split_done")
            pre_ready = sem("pre_ready")
            pre_taken = sem("pre_taken")
            e_ready = sem("e_ready")
            square_ready = sem("square_ready")
            series_ready = sem("series_ready")
            log_ready = sem("log_ready")
            soft_ready = sem("soft_ready")
            delta_ready = sem("delta_ready")
            dx_ready = sem("dx_ready")
            b_ready = sem("b_ready")
            c_ready = sem("c_ready")
            c_copied = sem("c_copied")
            decay_ready = sem("decay_ready")
            carry_in = sem("carry_in")
            drive_ready = sem("drive_ready")
            scan_done = sem("scan_done")
            carry_dve = sem("carry_dve")
            carry_pool = sem("carry_pool")
            limit_set = sem("limit_set")
            hc_dve = sem("hc_dve")
            hc_pool = sem("hc_pool")
            skip_added = sem("skip_added")
            reduced = sem("reduced")
            y_taken = sem("y_taken")
            y_stored = sem("y_stored")

            SMALL = 13

            def last_column(d):
                return T if d == 0 else 1

            def carry_column(d):
                return 0 if d == 0 else SEG - 1

            def run(eng, unit):
                unit(0, 0, True)
                unit(0, 1, False)
                with eng.Fori(1, NCH) as i:
                    unit(i, 0, False)
                    unit(i, 1, False)

            block = one.enter_context(nc.Block())

            @block.sync
            def _(sp):
                sp.dma_start(w_norm[:, :], norm_w).then_inc(s_small, 16)
                sp.dma_start(w_in[:, :, :], in_w.rearrange("(k p) e -> p k e", p=P)).then_inc(s_small, 16)
                sp.dma_start(xb[:, :, :], x_chunk[0, :, :, :]).then_inc(x_loaded, 16)
                for d in (0, 1):
                    sp.dma_start(taps[:, d, :, :], conv_w[d]).then_inc(s_small, 16)
                    sp.dma_start(b_conv[:, d, :], conv_b[d]).then_inc(s_small, 16)
                    sp.dma_start(skip[:, d, :], d_skip[d]).then_inc(s_small, 16)
                    sp.dma_start(b_dt[:, d, :], dt_b[d]).then_inc(s_small, 16)
                    sp.dma_start(neg_a[:, d, :, :], a_log[d]).then_inc(s_small, 16)
                sp.dma_start(w_dt[:, :, :], dt_w.rearrange("d r e -> r d e")).then_inc(s_small, 16)
                sp.wait_ge(s_xpad, 1)
                for d in (0, 1):
                    w = xproj_w[d].rearrange("(t p) e -> p t e", p=P)
                    sp.dma_start(w_x[:, d, :, 0:RANK], w[:, :, 0:RANK]).then_inc(s_xproj, 16)
                    for q in (1, 2, 3):
                        sp.dma_start(w_x[:, d, :, 32 * q:32 * q + 32], w[:, :, RANK:RANK + 2 * NS]).then_inc(s_xproj, 16)

                sp.wait_ge(xT_ready, 2)
                sp.dma_start(xb[:, :, :], x_chunk[rank_of_backward(0), :, :, :]).then_inc(x_loaded, 16)

                def unit(i, d, first):
                    u = 2 * i + d
                    j = (i + 1) % NCH if isinstance(i, int) else (i + 1) & (NCH - 1)
                    hold(sp, xT_ready, 2 * (u + 1) + 2, spare)
                    sp.dma_start(xb[:, :, :], x_chunk[j if d == 0 else rank_of_backward(j), :, :, :]).then_inc(x_loaded, 16)
                    if not first:
                        hold(sp, y_taken, u, spare)
                        c = i if d == 1 else rank_of_backward(i - 1)
                        sp.dma_start(y_dram[1 - d][c, :, :], ys[:, :, :].rearrange("p t n -> p (t n)")).then_inc(y_stored, 16)
                    if d == 1:
                        hold(sp, sz_ready, i + 2, spare)
                        sp.dma_start(z_dram[j, :, :], sz[:, :, :].rearrange("p t n -> p (t n)")).then_inc(sz_stored, 16)

                sp.wait_ge(sz_ready, 1)
                sp.dma_start(z_dram[0, :, :], sz[:, :, :].rearrange("p t n -> p (t n)")).then_inc(sz_stored, 16)
                run(sp, unit)
                sp.wait_ge(y_taken, 2 * NCH)
                sp.dma_start(y_dram[1][rank_of_backward(NCH - 1), :, :], ys[:, :, :].rearrange("p t n -> p (t n)")).then_inc(y_stored, 16)
                sp.wait_ge(y_stored, 16 * 2 * NCH)
                sp.wait_ge(sz_stored, 16 * (NCH + 1))
                sp.wait_ge(x_loaded, 16 * (2 * NCH + 2))

            @block.tensor
            def _(pe):
                w = work

                def project(slot, p, d, j):
                    q = XDBL
                    if slot == 0:
                        pe.wait_ge(xn_done, p + 1)
                        if d == 1 or not (isinstance(j, int) and j == 0):
                            pe.wait_ge(z_taken, 4 * (j + d))
                        wait(pe, pre_taken, 4 * p)
                        for k in range(KC):
                            for t in range(TT):
                                last = nc.tensor.transpose(w[k][:, t * P:(t + 1) * P], xb[:, t, k * P:(k + 1) * P], ident[:, :])
                            last.then_inc(xT_ready, 1)
                    if slot in (1, 2):
                        for m in (2 * slot - 2, 2 * slot - 1):
                            if m == 0:
                                pe.wait_ge(xT_taken, 2 * p + 2)
                            if m >= 2:
                                pe.wait_ge(xi_taken, 4 * p + m - 1)
                            for k in range(KC):
                                last = nc.tensor.matmul(w[m % 2][:, :], w_in[:, k, m * P:(m + 1) * P], xnT[:, k, :],
                                                        start=(k == 0), stop=(k == KC - 1))
                            last.then_inc(xi_ready, 1)
                    if slot in (4, 5, 6, 7):
                        for m in (slot - 4,):
                            if m == 0:
                                pe.wait_ge(xi_taken, 4 * p + 4)
                            if m >= 2:
                                pe.wait_ge(conv_taken, 4 * p + m - 1)
                            for k in range(TAPS):
                                at = k if d == 0 else HALO - k
                                last = nc.tensor.matmul(w[m % 2][:, :], tap_diag[:, d, m, k, :], xi[:, d, m, at:at + T],
                                                        start=(k == 0), stop=(k == TAPS - 1))
                            last.then_inc(conv_ready, 1)
                    if slot == q:
                        pe.wait_ge(silu_done, p + 1)
                        for m in range(CT):
                            last = nc.tensor.matmul(w[0][:, :], w_x[:, d, m, :], xc[:, m, :], start=(m == 0), stop=(m == CT - 1))
                        last.then_inc(xdbl_ready, 1)
                    if slot in (q + 1, q + 2):
                        for m in (2 * (slot - q) - 2, 2 * (slot - q) - 1):
                            if m == 0:
                                pe.wait_ge(dt_taken, p + 1)
                            if m == 1:
                                pe.wait_ge(rest_ready, p + 1)
                            if m >= 2:
                                pe.wait_ge(pre_taken, 4 * p + m - 1)
                            last = nc.tensor.matmul(w[(m + 1) % 2][:, :], w_dt[:, d, m * P:(m + 1) * P], dt_in[:, :], start=True, stop=True)
                            last.then_inc(pre_ready, 1)
                    if slot in (q + 3, q + 4, q + 5, q + 6) and d == 0:
                        m = slot - q - 3
                        if m < 2:
                            pe.wait_ge(pre_taken, 4 * p + 4)
                        else:
                            pe.wait_ge(z_taken, 4 * j + m - 1)
                        for k in range(KC):
                            last = nc.tensor.matmul(w[m % 2][:, :], w_in[:, k, DI + m * P:DI + (m + 1) * P], xnT[:, k, :],
                                                    start=(k == 0), stop=(k == KC - 1))
                        last.then_inc(z_ready, 1)

                def reduce(u, m):
                    if m in ON_DVE:
                        pe.wait_ge(hc_dve, N_DVE * u + before(m, True) + 1)
                    else:
                        pe.wait_ge(hc_pool, N_POOL * u + before(m, False) + 1)
                    for t in range(CT):
                        last = nc.tensor.matmul(y_ps[:, t, :], ident[:, :], state[:, m % RING, t, 1:T + 1], start=False, stop=(m == NS - 1))
                    last.then_inc(reduced, 1)

                def unit(i, d, first):
                    u = 2 * i + d
                    for n in range(NS):
                        wait(pe, drive_ready, 16 * u + n)
                        if n == 0:
                            pe.wait_ge(split_done, u + 1)
                        nc.tensor.matmul(b_ps[:, :], row_sel[:, n:n + 1].to_broadcast([P, P]), parts[:, d, :],
                                         start=True, stop=True).then_inc(b_ready, 1)
                        if (n - 1) in ON_DVE:
                            pe.wait_ge(hc_dve, N_DVE * u + before(n, True))
                        else:
                            wait(pe, c_copied, N_POOL * u + before(n, False))
                        nc.tensor.matmul(c_ps[:, :], row_sel[:, NS + n:NS + n + 1].to_broadcast([P, P]), parts[:, d, :],
                                         start=True, stop=True).then_inc(c_ready, 1)
                        if n < LAG and not first:
                            reduce(u - 1, NS - LAG + n)
                        if n == LAG:
                            wait(pe, y_taken, u)
                            for t in range(CT):
                                last = nc.tensor.matmul(y_ps[:, t, :], skip_diag[:, d, t, :], xc[:, t, :], start=True, stop=False)
                            last.then_inc(skip_added, 1)
                        if n >= LAG:
                            reduce(u, n - LAG)
                        project(n, u + 1, 1 - d, i + d)

                pe.wait_ge(s_ident, 2)
                pe.wait_ge(s_small, 16 * SMALL)
                pe.wait_ge(s_diags, 1)
                pe.wait_ge(s_xproj, 16 * 8)
                pe.wait_ge(s_sel, 4)
                for slot in range(NS):
                    project(slot, 0, 0, 0)
                run(pe, unit)
                for m in range(NS - LAG, NS):
                    reduce(2 * NCH - 1, m)

            @block.scalar
            def _(act):
                def normalise(p):
                    act.wait_ge(x_loaded, 16 * (p + 1))
                    wait(act, xn_done, p)
                    for t in range(TT):
                        last = nc.scalar.activation(junk[:, t, :], xb[:, t, :], ACT.Square, accum_out=sq[:, t:t + 1])
                    last.then_inc(sq_done, 1)

                def project(slot, p, d, j):
                    q = XDBL
                    if slot == 1:
                        for k in range(KC):
                            act.wait_ge(xT_ready, 2 * p + k + 1)
                            nc.scalar.activation(xnT[:, k, :], work[k][:, :], ACT.Copy, scale=w_norm[:, k:k + 1]).then_inc(xT_taken, 1)
                    if slot in (2, 3):
                        for m in (2 * slot - 4, 2 * slot - 3):
                            act.wait_ge(xi_ready, 4 * p + m + 1)
                            if m == 0:
                                wait(act, halo_moved, p - 1)
                            at = HALO if d == 0 else 0
                            nc.scalar.activation(xi[:, d, m, at:at + T], work[m % 2][:, :], ACT.Copy).then_inc(xi_taken, 1)
                    if slot in (5, 6, 7, 8):
                        for m in (slot - 5,):
                            act.wait_ge(conv_ready, 4 * p + m + 1)
                            if m == 0:
                                wait(act, skip_added, p)
                            nc.scalar.activation(xc[:, m, :], work[m % 2][:, :], ACT.Identity, bias=b_conv[:, d, m:m + 1]).then_inc(conv_taken, 1)
                    if slot == q:
                        act.wait_ge(conv_taken, 4 * p + 4)
                        nc.scalar.activation(xc[:, :, :], xc[:, :, :], ACT.Silu).then_inc(silu_done, 1)
                    if slot == q + 1:
                        act.wait_ge(xdbl_ready, p + 1)
                        nc.scalar.activation(parts[:, d, :], work[0][:, :], ACT.Copy).then_inc(high_ready, 1)
                        nc.scalar.activation(dt_in[:, :], work[0][0:RANK, :], ACT.Copy).then_inc(dt_taken, 1)
                    if slot in (q + 2, q + 3):
                        for m in (2 * (slot - q) - 4, 2 * (slot - q) - 3):
                            act.wait_ge(pre_ready, 4 * p + m + 1)
                            if m == 0:
                                wait(act, delta_ready, p)
                            nc.scalar.activation(ebuf[:, m, :], work[(m + 1) % 2][:, :], ACT.Abs, bias=b_dt[:, d, m:m + 1])
                            nc.scalar.activation(delta[:, d, m, :], work[(m + 1) % 2][:, :], ACT.Relu, bias=b_dt[:, d, m:m + 1]).then_inc(pre_taken, 1)
                    if slot == q + 3:
                        act.wait_ge(pre_taken, 4 * p + 4)
                        nc.scalar.activation(ebuf[:, :, :], ebuf[:, :, :], ACT.Exp, scale=-1.0).then_inc(e_ready, 1)
                        act.wait_ge(e_ready, p + 1)
                        nc.scalar.activation(series[:, :, :], ebuf[:, :, :], ACT.Square, scale=SERIES_A, bias=series_b[:, 0:1]).then_inc(square_ready, 1)
                    if slot == q + 5:
                        act.wait_ge(series_ready, p + 1)
                        nc.scalar.activation(ebuf[:, :, :], ebuf[:, :, :], ACT.Ln, bias=1.0).then_inc(log_ready, 1)
                    if slot in (q + 4, q + 5, q + 6, q + 7) and d == 0:
                        for m in (slot - q - 4,):
                            act.wait_ge(z_ready, 4 * j + m + 1)
                            if m == 0:
                                wait(act, sz_stored, 16 * j)
                            nc.scalar.activation(sz[:, m, :], work[m % 2][:, :], ACT.Copy).then_inc(z_taken, 1)
                    if slot == q + 7 and d == 0:
                        act.wait_ge(z_taken, 4 * j + 4)
                        nc.scalar.activation(sz[:, :, :], sz[:, :, :], ACT.Silu).then_inc(sz_ready, 1)

                def unit(i, d, first):
                    u = 2 * i + d
                    for n in range(NS):
                        if n == 0:
                            act.wait_ge(delta_ready, u + 1)
                        wait(act, scan_done, 16 * u + n - 1)
                        for t in range(CT):
                            last = nc.scalar.activation(decay[:, n % 2, t, 1:T + 1], delta[:, d, t, :], ACT.Exp, scale=neg_a[:, d, t, n:n + 1])
                        last.then_inc(decay_ready, 1)
                        if not (isinstance(i, int) and i == 0):
                            if n in ON_DVE:
                                act.wait_ge(carry_dve, N_DVE * (u - 2) + before(n, True) + 1)
                            else:
                                act.wait_ge(carry_pool, N_POOL * (u - 2) + before(n, False) + 1)
                        if not (first and n < RING):
                            act.wait_ge(reduced, 16 * u + n - RING + 1)
                        nc.scalar.activation(state[:, n % RING, :, carry_column(d)], carry[:, d, n, :], ACT.Copy).then_inc(carry_in, 1)
                        if n == LAG and not first:
                            act.wait_ge(reduced, 16 * u)
                            wait(act, y_stored, 16 * (u - 1))
                            nc.scalar.activation(ys[:, :, :], y_ps[:, :, :], ACT.Copy).then_inc(y_taken, 1)
                        if n not in ON_DVE:
                            c = N_POOL * u + before(n, False)
                            act.wait_ge(c_ready, 16 * u + n + 1)
                            if not (first and before(n, False) < 2):
                                act.wait_ge(hc_pool, c - 1)
                            nc.scalar.activation(c_sb[:, before(n, False) % 2, :], c_ps[:, :], ACT.Copy).then_inc(c_copied, 1)
                        if n == 12:
                            normalise(u + 2)
                        project(n, u + 1, 1 - d, i + d)

                act.wait_ge(s_small, 16 * SMALL)
                nc.scalar.activation(neg_a[:, :, :, :], neg_a[:, :, :, :], ACT.Exp).then_inc(s_aexp, 1)
                act.wait_ge(s_nega, 1)
                act.wait_ge(s_zeroed, 6)
                normalise(0)
                for slot in range(NS):
                    project(slot, 0, 0, 0)
                normalise(1)
                run(act, unit)
                act.wait_ge(reduced, 16 * 2 * NCH)
                act.wait_ge(y_stored, 16 * (2 * NCH - 1))
                nc.scalar.activation(ys[:, :, :], y_ps[:, :, :], ACT.Copy).then_inc(y_taken, 1)

            @block.vector
            def _(dve):
                def normalise(p):
                    dve.wait_ge(rstd_done, p + 1)
                    for t in range(TT):
                        last = nc.vector.tensor_scalar(xb[:, t, :], xb[:, t, :], rstd[:, t:t + 1], None, ALU.mult)
                    last.then_inc(xn_done, 1)

                def project(slot, p, d, j):
                    q = XDBL
                    if slot == 8:
                        dve.wait_ge(conv_ready, 4 * p + 4)
                        src, dst = (T, 0) if d == 0 else (0, T)
                        nc.vector.tensor_scalar(xi[:, d, :, dst:dst + HALO], xi[:, d, :, src:src + HALO],
                                                limits[:, 0, bass.ds(j, 1)], limits[:, 1, bass.ds(j, 1)], ALU.min, ALU.max).then_inc(halo_moved, 1)
                    if slot == q + 1:
                        dve.wait_ge(high_ready, p + 1)
                        nc.vector.tensor_tensor(out=part_f[64:128, :], in0=work[0][64:128, :], in1=parts[64:128, d, :], op=ALU.subtract).then_inc(rest_ready, 1)
                        dve.wait_ge(rest_ready, p + 1)
                        nc.vector.tensor_copy(parts[64:96, d, :], part_f[64:96, :])
                        nc.vector.tensor_copy(part_m[96:128, :], part_f[96:128, :]).then_inc(mid_ready, 1)
                        dve.wait_ge(mid_ready, p + 1)
                        nc.vector.tensor_tensor(out=parts[96:128, d, :], in0=part_f[96:128, :], in1=part_m[96:128, :], op=ALU.subtract).then_inc(split_done, 1)
                    if slot == q + 4:
                        dve.wait_ge(square_ready, p + 1)
                        nc.vector.scalar_tensor_tensor(out=series[:, :, :], in0=series[:, :, :], scalar=SERIES_C, in1=ebuf[:, :, :],
                                                       op0=ALU.add, op1=ALU.mult).then_inc(series_ready, 1)
                    if slot == q + 5:
                        dve.wait_ge(log_ready, p + 1)
                        nc.vector.scalar_tensor_tensor(out=ebuf[:, :, :], in0=ebuf[:, :, :], scalar=LOG_MARGIN, in1=series[:, :, :],
                                                       op0=ALU.add, op1=ALU.min).then_inc(soft_ready, 1)

                def unit(i, d, first):
                    u = 2 * i + d
                    for n in range(NS):
                        if n == 0:
                            dve.wait_ge(dx_ready, u + 1)
                        dve.wait_ge(b_ready, 16 * u + n + 1)
                        if not (first and n < RING):
                            dve.wait_ge(reduced, 16 * u + n - RING + 1)
                        nc.vector.tensor_tensor(out=state[:, n % RING, :, 1:T + 1], in0=dx[:, d, :, :],
                                                in1=b_ps[:, :].unsqueeze(1).to_broadcast([P, CT, T]), op=ALU.mult).then_inc(drive_ready, 1)
                        dve.wait_ge(drive_ready, 16 * u + n + 1)
                        dve.wait_ge(decay_ready, 16 * u + n + 1)
                        dve.wait_ge(carry_in, 16 * u + n + 1)
                        step = slice(None, None, 1 if d == 0 else -1)
                        a = decay[:, n % 2, :, :].rearrange("p t n -> p (t n)")[:, step]
                        b = state[:, n % RING, :, :].rearrange("p t n -> p (t n)")[:, step]
                        nc.vector.tensor_tensor_scan(b, a, b, 0.0, ALU.mult, ALU.add).then_inc(scan_done, 1)
                        if n in ON_DVE:
                            dve.wait_ge(scan_done, 16 * u + n + 1)
                            dve.wait_ge(c_ready, 16 * u + n + 1)
                            if n == ON_DVE[0]:
                                dve.wait_ge(limit_set, u + 1)
                            nc.vector.tensor_scalar(carry[:, d, n, :], state[:, n % RING, :, last_column(d)],
                                                    limit_now[:, d, 0:1], limit_now[:, d, 1:2], ALU.min, ALU.max).then_inc(carry_dve, 1)
                            dve.wait_ge(carry_dve, N_DVE * u + before(n, True) + 1)
                            nc.vector.tensor_tensor(out=state[:, n % RING, :, 1:T + 1], in0=state[:, n % RING, :, 1:T + 1],
                                                    in1=c_ps[:, :].unsqueeze(1).to_broadcast([P, CT, T]), op=ALU.mult).then_inc(hc_dve, 1)
                        if n == 4:
                            dve.wait_ge(carry_pool, N_POOL * u + 1)
                            nc.vector.tensor_copy(limit_now[:, 1 - d, :], limits[:, :, bass.ds(i + d, 1)].rearrange("p a o -> p (a o)")).then_inc(limit_set, 1)
                        if n == 14:
                            normalise(u + 2)
                        project(n, u + 1, 1 - d, i + d)

                dve.wait_ge(s_ident, 2)
                dve.wait_ge(s_small, 16 * SMALL)
                for d in (0, 1):
                    for t in range(CT):
                        for k in range(TAPS):
                            nc.vector.tensor_scalar(tap_diag[:, d, t, k, :], ident[:, :], taps[:, d, t, k:k + 1], None, ALU.mult)
                        last = nc.vector.tensor_scalar(skip_diag[:, d, t, :], ident[:, :], skip[:, d, t:t + 1], None, ALU.mult)
                last.then_inc(s_diags, 1)
                dve.wait_ge(s_aexp, 1)
                nc.vector.tensor_scalar(neg_a[:, :, :, :], neg_a[:, :, :, :], -1.0, None, ALU.mult).then_inc(s_nega, 1)
                dve.wait_ge(s_zeroed, 6)
                nc.vector.tensor_copy(limit_now[:, 0, :], limits[:, :, 0]).then_inc(limit_set, 1)
                normalise(0)
                for slot in range(NS):
                    project(slot, 0, 0, 0)
                normalise(1)
                run(dve, unit)

            @block.gpsimd
            def _(pool):
                def normalise(p):
                    hold(pool, sq_done, p + 1, spare)
                    nc.gpsimd.tensor_scalar(rstd[:, :], sq[:, :], 1.0 / DM, EPS, ALU.mult, ALU.add).then_inc(rstd_mid, 1)
                    pool.wait_ge(rstd_mid, p + 1)
                    nc.gpsimd.tensor_tensor(out=rstd[:, :], in0=rstd[:, :], in1=half_power[:, :], op=ALU.pow).then_inc(rstd_done, 1)

                def project(slot, p, d, j):
                    q = XDBL
                    if slot == q + 5:
                        pool.wait_ge(soft_ready, p + 1)
                        nc.gpsimd.tensor_tensor(out=delta[:, d, :, :], in0=delta[:, d, :, :], in1=ebuf[:, :, :], op=ALU.add).then_inc(delta_ready, 1)
                    if slot == q + 6:
                        pool.wait_ge(delta_ready, p + 1)
                        nc.gpsimd.tensor_tensor(out=dx[:, d, :, :], in0=delta[:, d, :, :], in1=xc[:, :, :], op=ALU.mult).then_inc(dx_ready, 1)

                def unit(i, d, first):
                    u = 2 * i + d
                    pool.wait_ge(limit_set, u + 1)
                    for n in range(NS):
                        if n not in ON_DVE:
                            c = N_POOL * u + before(n, False)
                            hold(pool, scan_done, 16 * u + n + 1, spare)
                            nc.gpsimd.tensor_scalar(carry[:, d, n, :], state[:, n % RING, :, last_column(d)],
                                                    limit_now[:, d, 0:1], limit_now[:, d, 1:2], ALU.min, ALU.max).then_inc(carry_pool, 1)
                            pool.wait_ge(c_copied, c + 1)
                            pool.wait_ge(carry_pool, c + 1)
                            nc.gpsimd.tensor_tensor(out=state[:, n % RING, :, 1:T + 1], in0=state[:, n % RING, :, 1:T + 1],
                                                    in1=c_sb[:, before(n, False) % 2, :].unsqueeze(1).to_broadcast([P, CT, T]), op=ALU.mult).then_inc(hc_pool, 1)
                        if n == 13:
                            normalise(u + 2)
                        project(n, u + 1, 1 - d, i + d)

                nc.gpsimd.memset(w_x[:, :, :, :], 0.0).then_inc(s_xpad, 1)
                nc.gpsimd.memset(ident[:, :], 0.0).then_inc(s_ident, 1)
                nc.gpsimd.memset(row_sel[:, :], 0.0).then_inc(s_sel, 1)
                nc.gpsimd.memset(decay[:, :, :, :], 0.0).then_inc(s_zeroed, 1)
                nc.gpsimd.memset(state[:, :, :, :], 0.0).then_inc(s_zeroed, 1)
                nc.gpsimd.memset(xi[:, :, :, :], 0.0).then_inc(s_zeroed, 1)
                nc.gpsimd.memset(carry[:, :, :, :], 0.0).then_inc(s_zeroed, 1)
                nc.gpsimd.memset(half_power[:, :], -0.5)
                nc.gpsimd.memset(series_b[:, :], SERIES_B)
                nc.gpsimd.memset(limits[:, 0, :], HUGE)
                nc.gpsimd.memset(limits[:, 1, :], -HUGE).then_inc(s_zeroed, 1)
                pool.wait_ge(s_zeroed, 5)
                nc.gpsimd.memset(limits[:, :, CPB - 1:NCH:CPB], 0.0).then_inc(s_zeroed, 1)
                pool.wait_ge(s_ident, 1)
                nc.gpsimd.affine_select(out=ident[:, :], in_=ident[:, :], compare_op=ALU.not_equal, fill=1.0,
                                        base=0, pattern=[[-1, P]], channel_multiplier=1).then_inc(s_ident, 1)
                for q in (1, 2, 3):
                    pool.wait_ge(s_sel, q)
                    nc.gpsimd.affine_select(out=row_sel[:, :], in_=row_sel[:, :], compare_op=ALU.not_equal, fill=1.0,
                                            base=-32 * q, pattern=[[-1, 32]], channel_multiplier=1).then_inc(s_sel, 1)
                normalise(0)
                for slot in range(NS):
                    project(slot, 0, 0, 0)
                normalise(1)
                run(pool, unit)

        experts(nc, sem, x_chunk, out_chunk, y_dram, z_dram, out_w, gate_w, gate_b, expert_w, expert_b)


def experts(nc, sem, x_chunk, out_chunk, y_dram, z_dram, out_w, gate_w, gate_b, expert_w, expert_b):
    fp32 = mybir.dt.float32
    ALU, ACT, AX = mybir.AluOpType, mybir.ActivationFunctionType, mybir.AxisListType
    EP = NE // 2
    ITEMS = TT * EP + TT // 2
    ADDS = TT * NE + TT // 2
    BIAS_ITEM = 2 * EP
    BANKS = 3
    assert ITEMS % BANKS == 0
    LINKS = 23

    def adds_until(m):
        half, rest = divmod(m, ITEMS // 2)
        return half * (ADDS // 2) + (ADDS // 2 if rest == BIAS_ITEM else 2 * (rest + 1))

    with ExitStack() as two:
        def sb(name, shape, dt=fp32):
            return two.enter_context(nc.sbuf_tensor(name, shape, dt))

        def pb(name, shape):
            return two.enter_context(nc.psum_tensor(name, shape, fp32))

        ident = sb("ident2", [P, P])
        w_out = sb("w_out", [P, CT, DM])
        w_gate = sb("w_gate", [P, KC, NR])
        b_gate = sb("b_gate", [P, NR])
        w_exp = sb("w_exp", [P, KC, NE * DM])
        b_exp = sb("b_exp", [NE, DM])
        first_key = sb("first_key", [P, TT, NR])
        half_power = sb("half_power2", [P, TT])
        yf = sb("yf", [P, 2, CT, T])
        yb = sb("yb", [P, 2, CT, T])
        sz = sb("sz2", [P, 2, CT, T])
        xr = sb("xr", [P, 2, TT, DM])
        v = sb("v", [P, 2, TT, DM])
        x1T = sb("x1T", [P, 2, KC, T])
        stats = sb("stats", [P, 2, TT, 6])
        mv = sb("mv", [P, 2, TT, 2])
        rs = sb("rs", [P, 2, TT])
        lg = sb("lg", [P, TT, NR])
        pr = sb("pr", [P, TT, NR])
        left = sb("left", [P, TT, NR])
        key = sb("key", [P, TT, NR])
        hot1 = sb("hot1", [P, TT, NR])
        hot2 = sb("hot2", [P, TT, NR])
        red = sb("red", [P, 8, TT])
        cw = sb("cw", [P, 2, TT, NR])
        cwT = sb("cwT", [NE, T])

        pO = [pb(f"pO{k}", [P, T]) for k in (0, 1)]
        pT = [pb(f"pT{k}", [P, T]) for k in (0, 1)]
        pG = pb("pG", [P, T])
        pE = [pb(f"pE{k}", [P, T]) for k in range(BANKS)]

        spare2 = sem("spare2")
        w_loaded = sem("w2_loaded")
        made = sem("made2")
        in_loaded = [sem(f"in2_loaded{k}") for k in (0, 1)]
        summed = sem("summed")
        gated = sem("gated")
        proj_ready = sem("proj_ready")
        v_ready = sem("v_ready")
        stat_ready = [sem(f"stat_ready{k}") for k in (0, 1)]
        mv_ready = [sem(f"mv_ready{k}") for k in (0, 1)]
        rs_mid = [sem(f"rs_mid{k}") for k in (0, 1)]
        rs_ready = [sem(f"rs_ready{k}") for k in (0, 1)]
        norm_ready = [sem(f"norm_ready{k}") for k in (0, 1)]
        x1T_ready = sem("x1T_ready")
        x1T_taken = sem("x1T_taken")
        gate_ready = sem("gate_ready")
        lg_ready = sem("lg_ready")
        pr_ready = sem("pr_ready")
        router_step = sem("router_step")
        cwT_ready = sem("cwT_ready")
        cwT_taken = sem("cwT_taken")
        item_ready = sem("item_ready")
        added = sem("added")
        stored = sem("stored")

        def run(eng, body):
            body(0, 0)
            with eng.Fori(0, (NCH - 4) // 2) as g:
                body(2 * g + 1, 1)
                body(2 * g + 2, 0)
            for c in (NCH - 3, NCH - 2, NCH - 1):
                body(c, c % 2)

        def exists(c, ahead):
            return not isinstance(c, int) or c + ahead < NCH

        def loads_of(c, slot):
            return 64 * ((c - slot) // 2 + 1) if isinstance(c, int) else 32 * (c - slot) + 64

        block = two.enter_context(nc.Block())

        @block.sync
        def _(sp):
            def load(c, slot):
                for dst, src in ((yf, y_dram[0]), (yb, y_dram[1]), (sz, z_dram)):
                    sp.dma_start(dst[:, slot, :, :].rearrange("p t n -> p (t n)"), src[c, :, :]).then_inc(in_loaded[slot], 16)
                sp.dma_start(xr[:, slot, :, :], x_chunk[c, :, :, :]).then_inc(in_loaded[slot], 16)

            load(0, 0)
            sp.dma_start(w_out[:, :, :], out_w.rearrange("(k p) e -> p k e", p=P)).then_inc(w_loaded, 16)
            sp.dma_start(w_gate[:, :, :], gate_w.rearrange("(k p) e -> p k e", p=P)).then_inc(w_loaded, 16)
            sp.dma_start(b_gate[:, :], gate_b.partition_broadcast(P)).then_inc(w_loaded, 16)
            sp.dma_start(b_exp[:, :], expert_b).then_inc(w_loaded, 16)
            load(1, 1)
            for e in range(NE):
                sp.dma_start(w_exp[:, :, e * DM:(e + 1) * DM], expert_w[e].rearrange("(k p) e -> p k e", p=P)).then_inc(w_loaded, 16)
            sp.wait_ge(v_ready, 2)
            load(2, 0)

            def body(c, slot):
                if exists(c, 3):
                    hold(sp, v_ready, 2 * (c + 2), spare2)
                    load(c + 3, 1 - slot)
                hold(sp, norm_ready[1], c + 1, spare2)
                sp.dma_start(out_chunk[c, :, :, :], v[:, slot, :, :]).then_inc(stored, 16)

            run(sp, body)
            sp.wait_ge(stored, 16 * NCH)

        @block.gpsimd
        def _(pool):
            def gate(c, slot):
                pool.wait_ge(in_loaded[slot], loads_of(c, slot))
                nc.gpsimd.tensor_tensor(out=yf[:, slot, :, :], in0=yf[:, slot, :, :], in1=yb[:, slot, :, :], op=ALU.add).then_inc(summed, 1)
                pool.wait_ge(summed, c + 1)
                nc.gpsimd.tensor_tensor(out=yf[:, slot, :, :], in0=yf[:, slot, :, :], in1=sz[:, slot, :, :], op=ALU.mult).then_inc(gated, 1)

            def root(k, c, eps):
                hold(pool, mv_ready[k], c + 1, spare2)
                nc.gpsimd.tensor_scalar(rs[:, k, :], mv[:, k, :, 1], eps, None, ALU.add).then_inc(rs_mid[k], 1)
                pool.wait_ge(rs_mid[k], c + 1)
                nc.gpsimd.tensor_tensor(out=rs[:, k, :], in0=rs[:, k, :], in1=half_power[:, :], op=ALU.pow).then_inc(rs_ready[k], 1)

            def body(c, slot):
                if exists(c, 1):
                    root(0, c + 1, 4 * EPS)
                if exists(c, 2):
                    gate(c + 2, slot)
                root(1, c, EPS)

            nc.gpsimd.memset(ident[:, :], 0.0).then_inc(made, 1)
            nc.gpsimd.memset(half_power[:, :], -0.5)
            for e in range(NR):
                nc.gpsimd.memset(first_key[:, :, e], 16.0 - e)
            pool.wait_ge(made, 1)
            nc.gpsimd.affine_select(out=ident[:, :], in_=ident[:, :], compare_op=ALU.not_equal, fill=1.0,
                                    base=0, pattern=[[-1, P]], channel_multiplier=1).then_inc(made, 1)
            gate(0, 0)
            root(0, 0, 4 * EPS)
            gate(1, 1)
            run(pool, body)

        @block.tensor
        def _(pe):
            def project(c, slot):
                pe.wait_ge(gated, c + 1)
                wait(pe, v_ready, 2 * c)
                for t in range(TT):
                    for k in range(CT):
                        last = nc.tensor.matmul(pO[t // 2][:, (t % 2) * DM:(t % 2 + 1) * DM], yf[:, slot, k, t * P:(t + 1) * P], w_out[:, k, :],
                                                start=(k == 0), stop=(k == CT - 1))
                    if t % 2:
                        last.then_inc(proj_ready, 1)

            def transpose(c, slot):
                pe.wait_ge(norm_ready[0], c + 1)
                wait(pe, cwT_taken, c)
                for k in range(KC):
                    for t in range(TT):
                        last = nc.tensor.transpose(pT[k][:, t * P:(t + 1) * P], v[:, slot, t, k * P:(k + 1) * P], ident[:, :])
                    last.then_inc(x1T_ready, 1)

            def router(c, slot):
                pe.wait_ge(x1T_taken, 2 * c + 2)
                for t in range(TT):
                    for k in range(KC):
                        last = nc.tensor.matmul(pG[:, t * NR:(t + 1) * NR], x1T[:, slot, k, t * P:(t + 1) * P], w_gate[:, k, :],
                                                start=(k == 0), stop=(k == KC - 1))
                last.then_inc(gate_ready, 1)

            def free(c, m):
                if m >= BANKS:
                    pe.wait_ge(added, ADDS * c + adds_until(m - BANKS))
                elif not (isinstance(c, int) and c == 0):
                    pe.wait_ge(added, ADDS * (c - 1) + adds_until(m - BANKS + ITEMS))

            def pairs(c, slot, t):
                for e in range(EP):
                    m = (t // 2) * (ITEMS // 2) + (t % 2) * EP + e
                    free(c, m)
                    for k in range(KC):
                        last = nc.tensor.matmul(pE[m % BANKS][:, :], x1T[:, slot, k, t * P:(t + 1) * P], w_exp[:, k, e * 2 * DM:(e + 1) * 2 * DM],
                                                start=(k == 0), stop=(k == KC - 1))
                    last.then_inc(item_ready, 1)

            def biases(c, half):
                m = half * (ITEMS // 2) + BIAS_ITEM
                pe.wait_ge(cwT_taken, c + 1)
                free(c, m)
                for t in (0, 1):
                    at = (2 * half + t) * P
                    last = nc.tensor.matmul(pE[m % BANKS][:, t * DM:(t + 1) * DM], cwT[:, at:at + P], b_exp[:, :], start=True, stop=True)
                last.then_inc(item_ready, 1)

            def body(c, slot):
                more = exists(c, 1)
                if more:
                    project(c + 1, 1 - slot)
                pairs(c, slot, 0)
                pe.wait_ge(router_step, LINKS * (c + 1))
                for t in range(TT):
                    last = nc.tensor.transpose(pT[0][0:NE, t * P:(t + 1) * P], cw[:, slot, t, 0:NE], ident[:, :])
                last.then_inc(cwT_ready, 1)
                pairs(c, slot, 1)
                biases(c, 0)
                if more:
                    transpose(c + 1, 1 - slot)
                pairs(c, slot, 2)
                if more:
                    router(c + 1, 1 - slot)
                pairs(c, slot, 3)
                biases(c, 1)

            pe.wait_ge(w_loaded, 16 * (4 + NE))
            pe.wait_ge(made, 2)
            project(0, 0)
            transpose(0, 0)
            router(0, 0)
            run(pe, body)

        @block.scalar
        def _(act):
            def head(c, slot):
                for k in range(KC):
                    act.wait_ge(x1T_ready, 2 * c + k + 1)
                    nc.scalar.activation(x1T[:, slot, k, :], pT[k][:, :], ACT.Copy).then_inc(x1T_taken, 1)
                act.wait_ge(lg_ready, c + 1)
                nc.scalar.activation(pr[:, :, :], lg[:, :, :], ACT.Exp).then_inc(pr_ready, 1)

            def body(c, slot):
                act.wait_ge(cwT_ready, c + 1)
                wait(act, item_ready, ITEMS * c)
                nc.scalar.activation(cwT[:, :], pT[0][0:NE, :], ACT.Copy).then_inc(cwT_taken, 1)
                if exists(c, 1):
                    head(c + 1, 1 - slot)

            head(0, 0)
            run(act, body)

        @block.vector
        def _(dve):
            def residual(c, slot):
                for k in (0, 1):
                    dve.wait_ge(proj_ready, 2 * c + k + 1)
                    if k == 0 and not (isinstance(c, int) and c < 2):
                        dve.wait_ge(stored, 16 * (c - 1))
                    nc.vector.scalar_tensor_tensor(out=v[:, slot, 2 * k:2 * k + 2, :], in0=xr[:, slot, 2 * k:2 * k + 2, :], scalar=4.0,
                                                   in1=pO[k][:, :].rearrange("p (t e) -> p t e", e=DM), op0=ALU.mult, op1=ALU.add).then_inc(v_ready, 1)
                dve.wait_ge(v_ready, 2 * c + 2)

            def moments(k, c, slot):
                for t in range(TT):
                    last = nc.vector.bn_stats(stats[:, k, t, :], v[:, slot, t, :])
                last.then_inc(stat_ready[k], 1)
                hold(dve, stat_ready[k], c + 1, spare2)
                for t in range(TT):
                    last = nc.vector.bn_aggr(mv[:, k, t, :], stats[:, k, t, :])
                last.then_inc(mv_ready[k], 1)

            def norm(k, c, slot):
                dve.wait_ge(rs_ready[k], c + 1)
                for t in range(TT):
                    last = nc.vector.tensor_scalar(v[:, slot, t, :], v[:, slot, t, :], mv[:, k, t, 0:1], rs[:, k, t:t + 1], ALU.subtract, ALU.mult)
                last.then_inc(norm_ready[k], 1)

            def over(col):
                return red[:, col, :].unsqueeze(2).to_broadcast([P, TT, NR])

            def logits(c):
                dve.wait_ge(gate_ready, c + 1)
                nc.vector.tensor_tensor(out=lg[:, :, :], in0=pG[:, 0:TT * NR].rearrange("p (t e) -> p t e", e=NR),
                                        in1=b_gate[:, :].unsqueeze(1).to_broadcast([P, TT, NR]), op=ALU.add).then_inc(router_step, 1)
                dve.wait_ge(router_step, LINKS * c + 1)
                nc.vector.tensor_reduce(red[:, 0, :], lg[:, :, :], AX.X, ALU.max).then_inc(router_step, 1)
                dve.wait_ge(router_step, LINKS * c + 2)
                nc.vector.tensor_tensor(out=lg[:, :, :], in0=lg[:, :, :], in1=over(0), op=ALU.subtract).then_inc(lg_ready, 1)

            def weights(c, slot):
                n = [2]

                def step(ins):
                    n[0] += 1
                    ins.then_inc(router_step, 1)
                    dve.wait_ge(router_step, LINKS * c + n[0])

                dve.wait_ge(pr_ready, c + 1)
                step(nc.vector.tensor_reduce(red[:, 1, :], pr[:, :, :], AX.X, ALU.add))
                step(nc.vector.reciprocal(red[:, 1, :], red[:, 1, :]))
                step(nc.vector.tensor_tensor(out=pr[:, :, :], in0=pr[:, :, :], in1=over(1), op=ALU.mult))
                for r, (src, hot) in enumerate(((pr, hot1), (left, hot2))):
                    step(nc.vector.tensor_reduce(red[:, 2, :], src[:, :, :], AX.X, ALU.max))
                    step(nc.vector.tensor_tensor(out=key[:, :, :], in0=src[:, :, :], in1=over(2), op=ALU.is_equal))
                    step(nc.vector.tensor_tensor(out=key[:, :, :], in0=key[:, :, :], in1=first_key[:, :, :], op=ALU.mult))
                    step(nc.vector.tensor_reduce(red[:, 3, :], key[:, :, :], AX.X, ALU.max))
                    step(nc.vector.tensor_tensor(out=hot[:, :, :], in0=key[:, :, :], in1=over(3), op=ALU.is_equal))
                    if r == 0:
                        step(nc.vector.scalar_tensor_tensor(out=left[:, :, :], in0=hot1[:, :, :], scalar=-2.0, in1=pr[:, :, :], op0=ALU.mult, op1=ALU.add))
                step(nc.vector.tensor_tensor(out=hot1[:, :, :], in0=hot1[:, :, :], in1=hot2[:, :, :], op=ALU.add))
                step(nc.vector.tensor_tensor(out=cw[:, slot, :, :], in0=pr[:, :, :], in1=hot1[:, :, :], op=ALU.mult))
                step(nc.vector.tensor_reduce(red[:, 4, :], cw[:, slot, :, 0:NE], AX.X, ALU.add))
                step(nc.vector.tensor_scalar(red[:, 5, :], red[:, 4, :], 0.0, None, ALU.is_le))
                step(nc.vector.tensor_tensor(out=red[:, 4, :], in0=red[:, 4, :], in1=red[:, 5, :], op=ALU.add))
                step(nc.vector.reciprocal(red[:, 4, :], red[:, 4, :]))
                step(nc.vector.tensor_tensor(out=cw[:, slot, :, :], in0=cw[:, slot, :, :], in1=over(4), op=ALU.mult))
                assert n[0] == LINKS

            def add_pairs(c, slot, t):
                for e in range(NE):
                    m = (t // 2) * (ITEMS // 2) + (t % 2) * EP + e // 2
                    done = adds_until(m) - 2 + e % 2
                    dve.wait_ge(item_ready, ITEMS * c + m + 1)
                    if e:
                        dve.wait_ge(added, ADDS * c + done)
                    nc.vector.scalar_tensor_tensor(out=v[:, slot, t, :], in0=pE[m % BANKS][:, (e % 2) * DM:(e % 2 + 1) * DM],
                                                   scalar=cw[:, slot, t, e:e + 1], in1=v[:, slot, t, :], op0=ALU.mult, op1=ALU.add).then_inc(added, 1)

            def add_biases(c, slot, half):
                m = half * (ITEMS // 2) + BIAS_ITEM
                dve.wait_ge(item_ready, ITEMS * c + m + 1)
                dve.wait_ge(added, ADDS * c + adds_until(m) - 1)
                both = v[:, slot, 2 * half:2 * half + 2, :]
                nc.vector.tensor_tensor(out=both, in0=both, in1=pE[m % BANKS][:, :].rearrange("p (t e) -> p t e", e=DM), op=ALU.add).then_inc(added, 1)

            def body(c, slot):
                more = exists(c, 1)
                if more:
                    residual(c + 1, 1 - slot)
                    moments(0, c + 1, 1 - slot)
                add_pairs(c, slot, 0)
                if more:
                    norm(0, c + 1, 1 - slot)
                add_pairs(c, slot, 1)
                add_biases(c, slot, 0)
                add_pairs(c, slot, 2)
                if more:
                    logits(c + 1)
                add_pairs(c, slot, 3)
                add_biases(c, slot, 1)
                dve.wait_ge(added, ADDS * (c + 1))
                moments(1, c, slot)
                if more:
                    weights(c + 1, 1 - slot)
                norm(1, c, slot)

            dve.wait_ge(made, 2)
            dve.wait_ge(w_loaded, 16 * (4 + NE))
            residual(0, 0)
            moments(0, 0, 0)
            norm(0, 0, 0)
            logits(0)
            weights(0, 0)
            run(dve, body)


def kernel(**inputs):
    import numpy as np
    import concourse.bacc as bacc
    from concourse.bass_utils import run_bass_kernel_spmd as launch

    def channels(w):
        return np.ascontiguousarray(np.swapaxes(w.reshape((-1, P) + w.shape[1:]), 0, 1))

    a = {k.replace("L0_attn_", "").replace("L0_ffn_", ""): np.asarray(v) for k, v in inputs.items()}
    both = lambda name, f: np.stack([f(a[name + "_f"]), f(a[name + "_b"])])
    arrays = {
        "x": np.ascontiguousarray(a["x"].reshape(B * L, DM)),
        "in_w": np.ascontiguousarray(a["in_proj_w"].T),
        "out_w": np.ascontiguousarray(a["out_proj_w"].T),
        "norm_w": channels(a["norm_w"]),
        "conv_w": both("conv_w", lambda w: channels(w[:, 0, :])),
        "conv_b": both("conv_b", channels),
        "xproj_w": both("xproj_w", lambda w: np.ascontiguousarray(w.T)),
        "dt_w": both("dtproj_w", lambda w: np.ascontiguousarray(w.T)),
        "dt_b": both("dtproj_b", channels),
        "a_log": both("A_log", channels),
        "d_skip": both("D", channels),
        "gate_w": np.ascontiguousarray(a["gate_w"].T),
        "gate_b": a["gate_b"],
        "expert_w": a["expert_w"],
        "expert_b": a["expert_b"],
    }
    nc = bacc.Bacc("TRN2", target_bir_lowering=False, num_devices=1)
    aps = {k: nc.dram_tensor(f"in_{k}", v.shape, mybir.dt.from_np(v.dtype), kind="ExternalInput").ap() for k, v in arrays.items()}
    out = nc.dram_tensor("out", (B * L, DM), mybir.dt.float32, kind="ExternalOutput").ap()
    mamba_moe(nc, out=out, **aps)
    r = launch(nc, [{f"in_{k}": v for k, v in arrays.items()}], core_ids=[0])
    return r.results[0]["out"].reshape(B, L, DM)
```

```python
import concourse.bass as bass
from concourse import mybir
from contextlib import ExitStack

B, L, DM = 4, 2048, 256
DI, NS, TAPS, RANK = 512, 16, 4, 16
P = 128
T = 512
NCH = B * L // T
CPB = L // T
CT = DI // P
TT = T // P
KC = DM // P
HALO = TAPS - 1
SEG = T + 2
NE, NR = 8, 10
EPS = 1e-5
EXP_AND_LOG = "natural_log_exp_and_others"
HUGE = 3.0e38
SERIES_A, SERIES_B, SERIES_C = 3 ** -0.5, -(3 ** 0.5) / 4, 13 / 16
LOG_MARGIN = 8e-8
PE_TAPS = TAPS - 1
RING = 4
CONV_SLOT = (0, 1, 2, 3)
Z_SLOT, Z_BANK = (4, 5, 9, 9), (0, 1, 1, 0)
XDBL = 6
SILU_Z = 13
NORM = 3
TURN = 11
XI_SLOT = (12, 13, 14, 14)
DECAYS = 4
AHEAD = 2
LAG = 3


def wait(eng, sem, value):
    if not isinstance(value, int) or value > 0:
        eng.wait_ge(sem, value)


def hold(eng, sem, value, spare):
    eng.wait_ge(sem, value)
    eng.sem_inc(spare, 1)


def rank_of_backward(i):
    return (i & (NCH - CPB)) + (CPB - 1 - (i & (CPB - 1)))


def mamba_moe(nc, x, in_w, out_w, norm_w, conv_w, conv_b, xproj_w, dt_w, dt_b, a_log, d_skip,
              gate_w, gate_b, expert_w, expert_b, out):
    fp32, bf16 = mybir.dt.float32, mybir.dt.bfloat16
    ALU, ACT, AX = mybir.AluOpType, mybir.ActivationFunctionType, mybir.AxisListType

    y_dram = [nc.dram_tensor(f"y_dir{d}", [NCH, P, CT * T], fp32, kind="Internal").ap() for d in (0, 1)]
    z_dram = nc.dram_tensor("silu_z", [NCH, P, CT * T], fp32, kind="Internal").ap()
    x_chunk = x.rearrange("(c t p) e -> c p t e", t=TT, p=P)
    out_chunk = out.rearrange("(c t p) e -> c p t e", t=TT, p=P)

    ctx = ExitStack()
    with ctx:
        def sem(name):
            return ctx.enter_context(nc.semaphore(name))

        with ExitStack() as one:
            def sb(name, shape, dt=fp32):
                return one.enter_context(nc.sbuf_tensor(name, shape, dt))

            def pb(name, shape):
                return one.enter_context(nc.psum_tensor(name, shape, fp32))

            ident = sb("ident", [P, P])
            w_in = sb("w_in", [P, KC, 2 * DI])
            w_x = sb("w_x", [P, 2, CT, P])
            w_dt = sb("w_dt", [RANK, 2, DI])
            taps = sb("taps", [P, 2, CT, TAPS])
            tap_diag = sb("tap_diag", [P, 2, CT, PE_TAPS, P])
            skip = sb("skip", [P, 2, CT])
            b_conv = sb("b_conv", [P, 2, CT])
            b_dt = sb("b_dt", [P, 2, CT])
            w_norm = sb("w_norm", [P, KC])
            neg_a = sb("neg_a", [P, 2, CT, NS])
            row_sel = sb("row_sel", [P, 32], bf16)
            limits = sb("limits", [P, 2, NCH + 1])
            limit_now = sb("limit_now", [P, 2, 2])
            half_power = sb("half_power", [P, TT])
            xb = sb("xb", [P, TT, DM])
            sq = sb("sq", [P, TT])
            rstd = sb("rstd", [P, TT])
            xnT = sb("xnT", [P, KC, T])
            xi = sb("xi", [P, 2, CT, T + HALO])
            xc = sb("xc", [P, 2, CT, T])
            sz = sb("sz", [P, CT, T])
            parts = sb("parts", [P, 2, T], bf16)
            part_m = sb("part_m", [P, T], bf16)
            dt_in = sb("dt_in", [RANK, T])
            ebuf = sb("ebuf", [P, CT, T])
            series = sb("series", [P, CT, T])
            series_b = sb("series_b", [P, 1])
            delta = sb("delta", [P, 2, CT, T])
            dx = sb("dx", [P, 2, CT, T])
            decay = sb("decay", [P, DECAYS, CT, SEG])
            state = sb("state", [P, RING, CT, SEG])
            c_sb = sb("c_sb", [P, 2, T])
            carry = sb("carry", [P, 2, NS, CT])
            ys = sb("ys", [P, CT, T])

            y_ps = pb("y_ps", [P, CT, T])
            b_ps = pb("b_ps", [P, T])
            c_ps = pb("c_ps", [P, T])
            work = [pb(f"work{k}", [P, T]) for k in (0, 1)]

            spare = sem("spare")
            s_small = sem("s_small")
            s_xproj = sem("s_xproj")
            s_ident = sem("s_ident")
            s_sel = sem("s_sel")
            s_zeroed = sem("s_zeroed")
            s_diags = sem("s_diags")
            s_aexp = sem("s_aexp")
            s_nega = sem("s_nega")
            s_xpad = sem("s_xpad")
            x_loaded = sem("x_loaded")
            sq_done = sem("sq_done")
            rstd_mid = sem("rstd_mid")
            rstd_done = sem("rstd_done")
            xn_done = sem("xn_done")
            xT_ready = sem("xT_ready")
            xT_taken = sem("xT_taken")
            xi_ready = sem("xi_ready")
            xi_taken = sem("xi_taken")
            conv_ready = sem("conv_ready")
            conv_taken = sem("conv_taken")
            halo_moved = sem("halo_moved")
            z_ready = sem("z_ready")
            z_taken = sem("z_taken")
            silu_done = sem("silu_done")
            sz_ready = sem("sz_ready")
            sz_stored = sem("sz_stored")
            xdbl_ready = sem("xdbl_ready")
            high_ready = sem("high_ready")
            dt_taken = sem("dt_taken")
            rest_ready = sem("rest_ready")
            mid_ready = sem("mid_ready")
            split_done = sem("split_done")
            pre_ready = sem("pre_ready")
            pre_taken = sem("pre_taken")
            e_ready = sem("e_ready")
            square_ready = sem("square_ready")
            series_ready = sem("series_ready")
            log_ready = sem("log_ready")
            soft_ready = sem("soft_ready")
            delta_ready = sem("delta_ready")
            dx_ready = sem("dx_ready")
            b_ready = sem("b_ready")
            c_ready = sem("c_ready")
            c_copied = sem("c_copied")
            decay_ready = sem("decay_ready")
            carry_in = sem("carry_in")
            drive_ready = sem("drive_ready")
            scan_done = sem("scan_done")
            carry_out = sem("carry_out")
            limit_set = sem("limit_set")
            hc_ready = sem("hc_ready")
            skip_made = sem("skip_made")
            reduced = sem("reduced")
            y_taken = sem("y_taken")
            y_stored = sem("y_stored")

            SMALL = 13

            def last_column(d):
                return T if d == 0 else 1

            def carry_column(d):
                return 0 if d == 0 else SEG - 1

            def run(eng, unit):
                unit(0, 0, True)
                unit(0, 1, False)
                with eng.Fori(1, NCH) as i:
                    unit(i, 0, False)
                    unit(i, 1, False)

            def last_tap(d):
                return HALO if d == 0 else 0

            def tiles_at(slots, slot):
                return [m for m in range(CT) if slots[m] == slot]

            block = one.enter_context(nc.Block())

            @block.sync
            def _(sp):
                sp.dma_start(w_norm[:, :], norm_w).then_inc(s_small, 16)
                sp.dma_start(w_in[:, :, :], in_w.rearrange("(k p) e -> p k e", p=P)).then_inc(s_small, 16)
                sp.dma_start(xb[:, :, :], x_chunk[0, :, :, :]).then_inc(x_loaded, 16)
                for d in (0, 1):
                    sp.dma_start(taps[:, d, :, :], conv_w[d]).then_inc(s_small, 16)
                    sp.dma_start(b_conv[:, d, :], conv_b[d]).then_inc(s_small, 16)
                    sp.dma_start(skip[:, d, :], d_skip[d]).then_inc(s_small, 16)
                    sp.dma_start(b_dt[:, d, :], dt_b[d]).then_inc(s_small, 16)
                    sp.dma_start(neg_a[:, d, :, :], a_log[d]).then_inc(s_small, 16)
                sp.dma_start(w_dt[:, :, :], dt_w.rearrange("d r e -> r d e")).then_inc(s_small, 16)
                sp.wait_ge(s_xpad, 1)
                for d in (0, 1):
                    w = xproj_w[d].rearrange("(t p) e -> p t e", p=P)
                    sp.dma_start(w_x[:, d, :, 0:RANK], w[:, :, 0:RANK]).then_inc(s_xproj, 16)
                    for q in (1, 2, 3):
                        sp.dma_start(w_x[:, d, :, 32 * q:32 * q + 32], w[:, :, RANK:RANK + 2 * NS]).then_inc(s_xproj, 16)

                sp.wait_ge(xT_ready, 2)
                sp.dma_start(xb[:, :, :], x_chunk[rank_of_backward(0), :, :, :]).then_inc(x_loaded, 16)

                def unit(i, d, first):
                    u = 2 * i + d
                    j = (i + 1) % NCH if isinstance(i, int) else (i + 1) & (NCH - 1)
                    hold(sp, xT_ready, 2 * (u + 1) + 2, spare)
                    sp.dma_start(xb[:, :, :], x_chunk[j if d == 0 else rank_of_backward(j), :, :, :]).then_inc(x_loaded, 16)
                    if not first:
                        hold(sp, y_taken, u, spare)
                        c = i if d == 1 else rank_of_backward(i - 1)
                        sp.dma_start(y_dram[1 - d][c, :, :], ys[:, :, :].rearrange("p t n -> p (t n)")).then_inc(y_stored, 16)
                    if d == 1:
                        hold(sp, sz_ready, i + 2, spare)
                        sp.dma_start(z_dram[j, :, :], sz[:, :, :].rearrange("p t n -> p (t n)")).then_inc(sz_stored, 16)

                sp.wait_ge(sz_ready, 1)
                sp.dma_start(z_dram[0, :, :], sz[:, :, :].rearrange("p t n -> p (t n)")).then_inc(sz_stored, 16)
                run(sp, unit)
                sp.wait_ge(y_taken, 2 * NCH)
                sp.dma_start(y_dram[1][rank_of_backward(NCH - 1), :, :], ys[:, :, :].rearrange("p t n -> p (t n)")).then_inc(y_stored, 16)
                sp.wait_ge(y_stored, 16 * 2 * NCH)
                sp.wait_ge(sz_stored, 16 * (NCH + 1))
                sp.wait_ge(x_loaded, 16 * (2 * NCH + 2))

            @block.tensor
            def _(pe):
                w = work

                def front(slot, p, d, z_tiles):
                    if slot == TURN:
                        pe.wait_ge(xn_done, p + 1)
                        wait(pe, pre_taken, 4 * p)
                        wait(pe, z_taken, z_tiles)
                        for k in range(KC):
                            for t in range(TT):
                                last = nc.tensor.transpose(w[k][:, t * P:(t + 1) * P], xb[:, t, k * P:(k + 1) * P], ident[:, :])
                            last.then_inc(xT_ready, 1)
                    for m in tiles_at(XI_SLOT, slot):
                        if m == 0:
                            pe.wait_ge(xT_taken, 2 * p + 2)
                        if m >= 2:
                            pe.wait_ge(xi_taken, 4 * p + m - 1)
                        for k in range(KC):
                            last = nc.tensor.matmul(w[m % 2][:, :], w_in[:, k, m * P:(m + 1) * P], xnT[:, k, :],
                                                    start=(k == 0), stop=(k == KC - 1))
                        last.then_inc(xi_ready, 1)

                def project(slot, p, d, j):
                    q = XDBL
                    for m in tiles_at(CONV_SLOT, slot):
                        if m == 0:
                            pe.wait_ge(xi_taken, 4 * p + 4)
                        if m >= 2:
                            pe.wait_ge(conv_taken, 4 * p + m - 1)
                        for k in range(PE_TAPS):
                            at = k if d == 0 else HALO - k
                            last = nc.tensor.matmul(w[m % 2][:, :], tap_diag[:, d, m, k, :], xi[:, d, m, at:at + T],
                                                    start=(k == 0), stop=(k == PE_TAPS - 1))
                        last.then_inc(conv_ready, 1)
                    if slot == q:
                        pe.wait_ge(silu_done, p + 1)
                        if d == 0:
                            pe.wait_ge(z_taken, 4 * j + 1)
                        for m in range(CT):
                            last = nc.tensor.matmul(w[0][:, :], w_x[:, d, m, :], xc[:, d, m, :], start=(m == 0), stop=(m == CT - 1))
                        last.then_inc(xdbl_ready, 1)
                    if slot in (q + 1, q + 2, q + 3):
                        for m in ((0,), (1, 2), (3,))[slot - q - 1]:
                            if m == 0:
                                pe.wait_ge(dt_taken, p + 1)
                                if d == 0:
                                    pe.wait_ge(z_taken, 4 * j + 2)
                            if m == 1:
                                pe.wait_ge(rest_ready, p + 1)
                            if m >= 2:
                                pe.wait_ge(pre_taken, 4 * p + m - 1)
                            last = nc.tensor.matmul(w[(m + 1) % 2][:, :], w_dt[:, d, m * P:(m + 1) * P], dt_in[:, :], start=True, stop=True)
                            last.then_inc(pre_ready, 1)
                    for m in tiles_at(Z_SLOT, slot) if d == 0 else ():
                        pe.wait_ge(*((conv_taken, 4 * p + 3), (conv_taken, 4 * p + 4), (pre_taken, 4 * p + 3), (pre_taken, 4 * p + 4))[m])
                        for k in range(KC):
                            last = nc.tensor.matmul(w[Z_BANK[m]][:, :], w_in[:, k, DI + m * P:DI + (m + 1) * P], xnT[:, k, :],
                                                    start=(k == 0), stop=(k == KC - 1))
                        last.then_inc(z_ready, 1)

                def reduce(u, m):
                    pe.wait_ge(hc_ready, NS * u + m + 1)
                    for t in range(CT):
                        last = nc.tensor.matmul(y_ps[:, t, :], ident[:, :], state[:, m % RING, t, 1:T + 1], start=(m == 0), stop=(m == NS - 1))
                    last.then_inc(reduced, 1)

                def unit(i, d, first):
                    u = 2 * i + d
                    for n in range(NS):
                        wait(pe, drive_ready, 16 * u + n)
                        if n == 0:
                            pe.wait_ge(split_done, u + 1)
                        nc.tensor.matmul(b_ps[:, :], row_sel[:, n:n + 1].to_broadcast([P, P]), parts[:, d, :],
                                         start=True, stop=True).then_inc(b_ready, 1)
                        wait(pe, c_copied, NS * u + n)
                        nc.tensor.matmul(c_ps[:, :], row_sel[:, NS + n:NS + n + 1].to_broadcast([P, P]), parts[:, d, :],
                                         start=True, stop=True).then_inc(c_ready, 1)
                        if n < LAG and not first:
                            reduce(u - 1, NS - LAG + n)
                        if n == LAG:
                            wait(pe, y_taken, u)
                        if n >= LAG:
                            reduce(u, n - LAG)
                        project(n, u + 1, 1 - d, i + d)
                        front(n, u + 2, d, 4 * (i + d + 1))

                pe.wait_ge(s_ident, 2)
                pe.wait_ge(s_small, 16 * SMALL)
                pe.wait_ge(s_diags, 1)
                pe.wait_ge(s_xproj, 16 * 8)
                pe.wait_ge(s_sel, 4)
                for slot in range(NS + 1):
                    front(slot, 0, 0, 0)
                for slot in range(NS):
                    project(slot, 0, 0, 0)
                for slot in range(NS + 1):
                    front(slot, 1, 1, 4)
                run(pe, unit)
                for m in range(NS - LAG, NS):
                    reduce(2 * NCH - 1, m)

            @block.scalar
            def _(act):
                def front(slot, p, d):
                    if slot == TURN:
                        for k in range(KC):
                            act.wait_ge(xT_ready, 2 * p + k + 1)
                            nc.scalar.activation(xnT[:, k, :], work[k][:, :], ACT.Copy, scale=w_norm[:, k:k + 1]).then_inc(xT_taken, 1)
                    for m in tiles_at(XI_SLOT, slot - 1):
                        act.wait_ge(xi_ready, 4 * p + m + 1)
                        if m == 0:
                            wait(act, halo_moved, p - 1)
                        at = HALO if d == 0 else 0
                        nc.scalar.activation(xi[:, d, m, at:at + T], work[m % 2][:, :], ACT.Copy).then_inc(xi_taken, 1)

                squares = series[:, 0:2, :].rearrange("p a (b e) -> p (a b) e", e=DM)

                def normalise(p):
                    act.wait_ge(x_loaded, 16 * (p + 1))
                    wait(act, xn_done, p)
                    wait(act, delta_ready, p - 1)
                    for t in range(TT):
                        last = nc.scalar.activation(squares[:, t, :], xb[:, t, :], ACT.Square, accum_out=sq[:, t:t + 1])
                    last.then_inc(sq_done, 1)

                def project(slot, p, d, j):
                    q = XDBL
                    if slot == q - 1:
                        act.wait_ge(conv_taken, 4 * p + 4)
                        for m in range(CT):
                            last = nc.scalar.activation(xc[:, d, m, :], xc[:, d, m, :], ACT.Silu, bias=b_conv[:, d, m:m + 1])
                        last.then_inc(silu_done, 1)
                        nc.scalar.preload_act_table_set(EXP_AND_LOG)
                    for m in tiles_at(Z_SLOT, slot - 1) if d == 0 else ():
                        act.wait_ge(z_ready, 4 * j + m + 1)
                        if m == 0:
                            wait(act, sz_stored, 16 * j)
                        nc.scalar.activation(sz[:, m, :], work[Z_BANK[m]][:, :], ACT.Copy).then_inc(z_taken, 1)
                    if slot == SILU_Z and d == 0:
                        act.wait_ge(z_taken, 4 * j + 4)
                        nc.scalar.activation(sz[:, :, :], sz[:, :, :], ACT.Silu).then_inc(sz_ready, 1)
                        nc.scalar.preload_act_table_set(EXP_AND_LOG)
                    if slot == q + 1:
                        act.wait_ge(xdbl_ready, p + 1)
                        nc.scalar.activation(parts[:, d, :], work[0][:, :], ACT.Copy).then_inc(high_ready, 1)
                        nc.scalar.activation(dt_in[:, :], work[0][0:RANK, :], ACT.Copy).then_inc(dt_taken, 1)
                    if slot in (q + 2, q + 3):
                        for m in (2 * (slot - q) - 4, 2 * (slot - q) - 3):
                            act.wait_ge(pre_ready, 4 * p + m + 1)
                            if m == 0:
                                wait(act, series_ready, p)
                            nc.scalar.activation(ebuf[:, m, :], work[(m + 1) % 2][:, :], ACT.Abs, bias=b_dt[:, d, m:m + 1])
                            nc.scalar.activation(delta[:, d, m, :], work[(m + 1) % 2][:, :], ACT.Relu, bias=b_dt[:, d, m:m + 1]).then_inc(pre_taken, 1)
                    if slot == q + 3:
                        act.wait_ge(pre_taken, 4 * p + 4)
                        nc.scalar.activation(ebuf[:, :, :], ebuf[:, :, :], ACT.Exp, scale=-1.0).then_inc(e_ready, 1)
                    if slot == q + 4:
                        act.wait_ge(e_ready, p + 1)
                        act.wait_ge(split_done, p + 1)
                        nc.scalar.activation(series[:, :, :], ebuf[:, :, :], ACT.Square, scale=SERIES_A, bias=series_b[:, 0:1]).then_inc(square_ready, 1)
                    if slot == q + 5:
                        wait(act, y_stored, 16 * (p - 1))
                        nc.scalar.activation(ys[:, :, :], ebuf[:, :, :], ACT.Ln, bias=1.0).then_inc(log_ready, 1)

                def make_decay(u, d, m, first):
                    if m == 0:
                        act.wait_ge(delta_ready, u + 1)
                    if not (first and m < DECAYS):
                        act.wait_ge(scan_done, 16 * u + m - DECAYS + 1)
                    for t in range(CT):
                        last = nc.scalar.activation(decay[:, m % DECAYS, t, 1:T + 1], delta[:, d, t, :], ACT.Exp, scale=neg_a[:, d, t, m:m + 1])
                    last.then_inc(decay_ready, 1)

                def unit(i, d, first):
                    u = 2 * i + d
                    for n in range(NS):
                        if n < NS - AHEAD:
                            make_decay(u, d, n + AHEAD, first)
                        if not (isinstance(i, int) and i == 0):
                            act.wait_ge(carry_out, NS * (u - 2) + n + 1)
                        if not (first and n < RING):
                            act.wait_ge(reduced, 16 * u + n - RING + 1)
                        nc.scalar.activation(state[:, n % RING, :, carry_column(d)], carry[:, d, n, :], ACT.Copy).then_inc(carry_in, 1)
                        act.wait_ge(c_ready, NS * u + n + 1)
                        if not (first and n < 2):
                            act.wait_ge(hc_ready, NS * u + n - 1)
                        nc.scalar.activation(c_sb[:, n % 2, :], c_ps[:, :], ACT.Copy).then_inc(c_copied, 1)
                        if n == NORM:
                            normalise(u + 2)
                        if n == NS - 1:
                            act.wait_ge(soft_ready, u + 2)
                            for t in range(CT):
                                last = nc.scalar.activation(ys[:, t, :], xc[:, d, t, :], ACT.Copy, scale=skip[:, d, t:t + 1])
                            last.then_inc(skip_made, 1)
                        project(n, u + 1, 1 - d, i + d)
                        front(n, u + 2, d)
                        if n >= NS - AHEAD:
                            make_decay(u + 1, 1 - d, n + AHEAD - NS, False)

                act.wait_ge(s_small, 16 * SMALL)
                nc.scalar.preload_act_table_set(EXP_AND_LOG)
                nc.scalar.activation(neg_a[:, :, :, :], neg_a[:, :, :, :], ACT.Exp).then_inc(s_aexp, 1)
                act.wait_ge(s_nega, 1)
                act.wait_ge(s_zeroed, 6)
                normalise(0)
                for slot in range(NS + 1):
                    front(slot, 0, 0)
                for slot in range(NS):
                    project(slot, 0, 0, 0)
                act.wait_ge(delta_ready, 1)
                normalise(1)
                for slot in range(NS + 1):
                    front(slot, 1, 1)
                for m in range(AHEAD):
                    make_decay(0, 0, m, True)
                run(act, unit)

            @block.vector
            def _(dve):
                def normalise(p):
                    dve.wait_ge(rstd_done, p + 1)
                    for t in range(TT):
                        last = nc.vector.tensor_scalar(xb[:, t, :], xb[:, t, :], rstd[:, t:t + 1], None, ALU.mult)
                    last.then_inc(xn_done, 1)

                def project(slot, p, d, j):
                    q = XDBL
                    for m in tiles_at(CONV_SLOT, slot):
                        dve.wait_ge(conv_ready, 4 * p + m + 1)
                        if m == 0:
                            wait(dve, skip_made, p - 1)
                            wait(dve, dx_ready, p - 1)
                        nc.vector.scalar_tensor_tensor(out=xc[:, d, m, :], in0=xi[:, d, m, last_tap(d):last_tap(d) + T], scalar=taps[:, d, m, TAPS - 1:TAPS],
                                                       in1=work[m % 2][:, :], op0=ALU.mult, op1=ALU.add).then_inc(conv_taken, 1)
                    if slot == 4:
                        dve.wait_ge(conv_taken, 4 * p + 4)
                        src, dst = (T, 0) if d == 0 else (0, T)
                        nc.vector.tensor_scalar(xi[:, d, :, dst:dst + HALO], xi[:, d, :, src:src + HALO],
                                                limits[:, 0, bass.ds(j, 1)], limits[:, 1, bass.ds(j, 1)], ALU.min, ALU.max).then_inc(halo_moved, 1)
                    if slot == q + 1:
                        dve.wait_ge(high_ready, p + 1)
                        wait(dve, delta_ready, p)
                        dve.wait_ge(sq_done, p + 1 if isinstance(p, int) and p == 0 else p + 2)
                        nc.vector.tensor_tensor(out=series[64:128, 0, :], in0=work[0][64:128, :], in1=parts[64:128, d, :], op=ALU.subtract).then_inc(rest_ready, 1)
                        dve.wait_ge(rest_ready, p + 1)
                        nc.vector.tensor_copy(parts[64:96, d, :], series[64:96, 0, :])
                        nc.vector.tensor_copy(part_m[96:128, :], series[96:128, 0, :]).then_inc(mid_ready, 1)
                        dve.wait_ge(mid_ready, p + 1)
                        nc.vector.tensor_tensor(out=parts[96:128, d, :], in0=series[96:128, 0, :], in1=part_m[96:128, :], op=ALU.subtract).then_inc(split_done, 1)
                    if slot == q + 5:
                        dve.wait_ge(square_ready, p + 1)
                        nc.vector.scalar_tensor_tensor(out=series[:, :, :], in0=series[:, :, :], scalar=SERIES_C, in1=ebuf[:, :, :],
                                                       op0=ALU.add, op1=ALU.mult).then_inc(series_ready, 1)
                    if slot == q + 6:
                        dve.wait_ge(series_ready, p + 1)
                        dve.wait_ge(log_ready, p + 1)
                        nc.vector.scalar_tensor_tensor(out=series[:, :, :], in0=ys[:, :, :], scalar=LOG_MARGIN, in1=series[:, :, :],
                                                       op0=ALU.add, op1=ALU.min).then_inc(soft_ready, 1)
                    if slot == q + 7:
                        dve.wait_ge(soft_ready, p + 1)
                        nc.vector.tensor_tensor(out=delta[:, d, :, :], in0=delta[:, d, :, :], in1=series[:, :, :], op=ALU.add).then_inc(delta_ready, 1)

                def take_y(u):
                    dve.wait_ge(reduced, 16 * u)
                    dve.wait_ge(skip_made, u)
                    nc.vector.tensor_tensor(out=ys[:, :, :], in0=ys[:, :, :], in1=y_ps[:, :, :], op=ALU.add).then_inc(y_taken, 1)

                def unit(i, d, first):
                    u = 2 * i + d
                    for n in range(NS):
                        if n == 0:
                            dve.wait_ge(dx_ready, u + 1)
                        dve.wait_ge(b_ready, 16 * u + n + 1)
                        if not (first and n < RING):
                            dve.wait_ge(reduced, 16 * u + n - RING + 1)
                        nc.vector.tensor_tensor(out=state[:, n % RING, :, 1:T + 1], in0=dx[:, d, :, :],
                                                in1=b_ps[:, :].unsqueeze(1).to_broadcast([P, CT, T]), op=ALU.mult).then_inc(drive_ready, 1)
                        if n == LAG - 1 and not first:
                            take_y(u)
                        dve.wait_ge(drive_ready, 16 * u + n + 1)
                        dve.wait_ge(decay_ready, 16 * u + n + 1)
                        dve.wait_ge(carry_in, 16 * u + n + 1)
                        step = slice(None, None, 1 if d == 0 else -1)
                        a = decay[:, n % DECAYS, :, :].rearrange("p t n -> p (t n)")[:, step]
                        b = state[:, n % RING, :, :].rearrange("p t n -> p (t n)")[:, step]
                        nc.vector.tensor_tensor_scan(b, a, b, 0.0, ALU.mult, ALU.add).then_inc(scan_done, 1)
                        if n == 4:
                            dve.wait_ge(carry_out, NS * u + 1)
                            nc.vector.tensor_copy(limit_now[:, 1 - d, :], limits[:, :, bass.ds(i + d, 1)].rearrange("p a o -> p (a o)")).then_inc(limit_set, 1)
                        if n == NORM + 4:
                            normalise(u + 2)
                        project(n, u + 1, 1 - d, i + d)

                dve.wait_ge(s_ident, 2)
                dve.wait_ge(s_small, 16 * SMALL)
                for d in (0, 1):
                    for t in range(CT):
                        for k in range(PE_TAPS):
                            last = nc.vector.tensor_scalar(tap_diag[:, d, t, k, :], ident[:, :], taps[:, d, t, k:k + 1], None, ALU.mult)
                last.then_inc(s_diags, 1)
                dve.wait_ge(s_aexp, 1)
                nc.vector.tensor_scalar(neg_a[:, :, :, :], neg_a[:, :, :, :], -1.0, None, ALU.mult).then_inc(s_nega, 1)
                dve.wait_ge(s_zeroed, 6)
                nc.vector.tensor_copy(limit_now[:, 0, :], limits[:, :, 0]).then_inc(limit_set, 1)
                normalise(0)
                for slot in range(NS):
                    project(slot, 0, 0, 0)
                normalise(1)
                run(dve, unit)
                take_y(2 * NCH)

            @block.gpsimd
            def _(pool):
                def normalise(p):
                    hold(pool, sq_done, p + 1, spare)
                    nc.gpsimd.tensor_scalar(rstd[:, :], sq[:, :], 1.0 / DM, EPS, ALU.mult, ALU.add).then_inc(rstd_mid, 1)
                    pool.wait_ge(rstd_mid, p + 1)
                    nc.gpsimd.tensor_tensor(out=rstd[:, :], in0=rstd[:, :], in1=half_power[:, :], op=ALU.pow).then_inc(rstd_done, 1)

                def project(slot, p, d, j):
                    q = XDBL
                    if slot == q + 8:
                        pool.wait_ge(delta_ready, p + 1)
                        nc.gpsimd.tensor_tensor(out=dx[:, d, :, :], in0=delta[:, d, :, :], in1=xc[:, d, :, :], op=ALU.mult).then_inc(dx_ready, 1)

                def unit(i, d, first):
                    u = 2 * i + d
                    pool.wait_ge(limit_set, u + 1)
                    for n in range(NS):
                        project(n, u + 1, 1 - d, i + d)
                        hold(pool, scan_done, NS * u + n + 1, spare)
                        nc.gpsimd.tensor_scalar(carry[:, d, n, :], state[:, n % RING, :, last_column(d)],
                                                limit_now[:, d, 0:1], limit_now[:, d, 1:2], ALU.min, ALU.max).then_inc(carry_out, 1)
                        pool.wait_ge(c_copied, NS * u + n + 1)
                        pool.wait_ge(carry_out, NS * u + n + 1)
                        nc.gpsimd.tensor_tensor(out=state[:, n % RING, :, 1:T + 1], in0=state[:, n % RING, :, 1:T + 1],
                                                in1=c_sb[:, n % 2, :].unsqueeze(1).to_broadcast([P, CT, T]), op=ALU.mult).then_inc(hc_ready, 1)
                        if n == NORM + 1:
                            normalise(u + 2)

                nc.gpsimd.memset(w_x[:, :, :, :], 0.0).then_inc(s_xpad, 1)
                nc.gpsimd.memset(ident[:, :], 0.0).then_inc(s_ident, 1)
                nc.gpsimd.memset(row_sel[:, :], 0.0).then_inc(s_sel, 1)
                nc.gpsimd.memset(decay[:, :, :, :], 0.0).then_inc(s_zeroed, 1)
                nc.gpsimd.memset(state[:, :, :, :], 0.0).then_inc(s_zeroed, 1)
                nc.gpsimd.memset(xi[:, :, :, :], 0.0).then_inc(s_zeroed, 1)
                nc.gpsimd.memset(carry[:, :, :, :], 0.0).then_inc(s_zeroed, 1)
                nc.gpsimd.memset(half_power[:, :], -0.5)
                nc.gpsimd.memset(series_b[:, :], SERIES_B)
                nc.gpsimd.memset(limits[:, 0, :], HUGE)
                nc.gpsimd.memset(limits[:, 1, :], -HUGE).then_inc(s_zeroed, 1)
                pool.wait_ge(s_zeroed, 5)
                nc.gpsimd.memset(limits[:, :, CPB - 1:NCH:CPB], 0.0).then_inc(s_zeroed, 1)
                pool.wait_ge(s_ident, 1)
                nc.gpsimd.affine_select(out=ident[:, :], in_=ident[:, :], compare_op=ALU.not_equal, fill=1.0,
                                        base=0, pattern=[[-1, P]], channel_multiplier=1).then_inc(s_ident, 1)
                for q in (1, 2, 3):
                    pool.wait_ge(s_sel, q)
                    nc.gpsimd.affine_select(out=row_sel[:, :], in_=row_sel[:, :], compare_op=ALU.not_equal, fill=1.0,
                                            base=-32 * q, pattern=[[-1, 32]], channel_multiplier=1).then_inc(s_sel, 1)
                normalise(0)
                for slot in range(NS):
                    project(slot, 0, 0, 0)
                normalise(1)
                run(pool, unit)

        experts(nc, sem, x_chunk, out_chunk, y_dram, z_dram, out_w, gate_w, gate_b, expert_w, expert_b)


def experts(nc, sem, x_chunk, out_chunk, y_dram, z_dram, out_w, gate_w, gate_b, expert_w, expert_b):
    fp32 = mybir.dt.float32
    ALU, ACT, AX = mybir.AluOpType, mybir.ActivationFunctionType, mybir.AxisListType
    EP = NE // 2
    ITEMS = TT * EP + TT // 2
    ADDS = TT * NE + TT // 2
    BIAS_ITEM = 2 * EP
    BANKS = 3
    assert ITEMS % BANKS == 0
    LINKS = 23

    def adds_until(m):
        half, rest = divmod(m, ITEMS // 2)
        return half * (ADDS // 2) + (ADDS // 2 if rest == BIAS_ITEM else 2 * (rest + 1))

    with ExitStack() as two:
        def sb(name, shape, dt=fp32):
            return two.enter_context(nc.sbuf_tensor(name, shape, dt))

        def pb(name, shape):
            return two.enter_context(nc.psum_tensor(name, shape, fp32))

        ident = sb("ident2", [P, P])
        w_out = sb("w_out", [P, CT, DM])
        w_gate = sb("w_gate", [P, KC, NR])
        b_gate = sb("b_gate", [P, NR])
        w_exp = sb("w_exp", [P, KC, NE * DM])
        b_exp = sb("b_exp", [NE, DM])
        first_key = sb("first_key", [P, TT, NR])
        half_power = sb("half_power2", [P, TT])
        yf = sb("yf", [P, 2, CT, T])
        yb = sb("yb", [P, 2, CT, T])
        sz = sb("sz2", [P, 2, CT, T])
        xr = sb("xr", [P, 2, TT, DM])
        v = sb("v", [P, 2, TT, DM])
        result = sb("result", [P, 2, TT, DM])
        x1T = sb("x1T", [P, 2, KC, T])
        stats = sb("stats", [P, 2, TT, 6])
        mv = sb("mv", [P, 2, TT, 2])
        rs = sb("rs", [P, 2, TT])
        lg = sb("lg", [P, TT, NR])
        pr = sb("pr", [P, TT, NR])
        left = sb("left", [P, TT, NR])
        key = sb("key", [P, TT, NR])
        hot1 = sb("hot1", [P, TT, NR])
        hot2 = sb("hot2", [P, TT, NR])
        red = sb("red", [P, 8, TT])
        cw = sb("cw", [P, 2, TT, NR])
        cwT = sb("cwT", [NE, T])

        pO = [pb(f"pO{k}", [P, T]) for k in (0, 1)]
        pT = [pb(f"pT{k}", [P, T]) for k in (0, 1)]
        pG = pb("pG", [P, T])
        pE = [pb(f"pE{k}", [P, T]) for k in range(BANKS)]

        spare2 = sem("spare2")
        w_loaded = sem("w2_loaded")
        made = sem("made2")
        in_loaded = [sem(f"in2_loaded{k}") for k in (0, 1)]
        summed = sem("summed")
        gated = sem("gated")
        proj_ready = sem("proj_ready")
        v_ready = sem("v_ready")
        stat_ready = [sem(f"stat_ready{k}") for k in (0, 1)]
        mv_ready = [sem(f"mv_ready{k}") for k in (0, 1)]
        rs_mid = [sem(f"rs_mid{k}") for k in (0, 1)]
        rs_ready = [sem(f"rs_ready{k}") for k in (0, 1)]
        norm_ready = [sem(f"norm_ready{k}") for k in (0, 1)]
        x1T_ready = sem("x1T_ready")
        x1T_taken = sem("x1T_taken")
        gate_ready = sem("gate_ready")
        lg_ready = sem("lg_ready")
        pr_ready = sem("pr_ready")
        router_step = sem("router_step")
        cwT_ready = sem("cwT_ready")
        cwT_taken = sem("cwT_taken")
        item_ready = sem("item_ready")
        added = sem("added")
        result_free = [sem(f"result_free{k}") for k in (0, 1)]

        def run(eng, body):
            body(0, 0)
            with eng.Fori(0, (NCH - 4) // 2) as g:
                body(2 * g + 1, 1)
                body(2 * g + 2, 0)
            for c in (NCH - 3, NCH - 2, NCH - 1):
                body(c, c % 2)

        def exists(c, ahead):
            return not isinstance(c, int) or c + ahead < NCH

        def loads_of(c, slot):
            return 64 * ((c - slot) // 2 + 1) if isinstance(c, int) else 32 * (c - slot) + 64

        block = two.enter_context(nc.Block())

        @block.sync
        def _(sp):
            for slot in (0, 1):
                sp.sem_inc(result_free[slot], 16)

            def load(c, slot):
                for dst, src in ((yf, y_dram[0]), (yb, y_dram[1]), (sz, z_dram)):
                    sp.dma_start(dst[:, slot, :, :].rearrange("p t n -> p (t n)"), src[c, :, :]).then_inc(in_loaded[slot], 16)
                sp.dma_start(xr[:, slot, :, :], x_chunk[c, :, :, :]).then_inc(in_loaded[slot], 16)

            load(0, 0)
            sp.dma_start(w_out[:, :, :], out_w.rearrange("(k p) e -> p k e", p=P)).then_inc(w_loaded, 16)
            sp.dma_start(w_gate[:, :, :], gate_w.rearrange("(k p) e -> p k e", p=P)).then_inc(w_loaded, 16)
            sp.dma_start(b_gate[:, :], gate_b.partition_broadcast(P)).then_inc(w_loaded, 16)
            sp.dma_start(b_exp[:, :], expert_b).then_inc(w_loaded, 16)
            load(1, 1)
            for e in range(NE):
                sp.dma_start(w_exp[:, :, e * DM:(e + 1) * DM], expert_w[e].rearrange("(k p) e -> p k e", p=P)).then_inc(w_loaded, 16)
            sp.wait_ge(v_ready, 2)
            load(2, 0)

            def body(c, slot):
                if exists(c, 3):
                    hold(sp, v_ready, 2 * (c + 2), spare2)
                    load(c + 3, 1 - slot)
                hold(sp, norm_ready[1], c + 1, spare2)
                sp.dma_start(out_chunk[c, :, :, :], result[:, slot, :, :]).then_inc(result_free[slot], 16)

            run(sp, body)
            for slot in (0, 1):
                sp.wait_ge(result_free[slot], 8 * NCH + 16)

        @block.gpsimd
        def _(pool):
            def gate(c, slot):
                pool.wait_ge(in_loaded[slot], loads_of(c, slot))
                nc.gpsimd.tensor_tensor(out=yf[:, slot, :, :], in0=yf[:, slot, :, :], in1=yb[:, slot, :, :], op=ALU.add).then_inc(summed, 1)
                pool.wait_ge(summed, c + 1)
                nc.gpsimd.tensor_tensor(out=yf[:, slot, :, :], in0=yf[:, slot, :, :], in1=sz[:, slot, :, :], op=ALU.mult).then_inc(gated, 1)

            def root(k, c, eps):
                hold(pool, mv_ready[k], c + 1, spare2)
                nc.gpsimd.tensor_scalar(rs[:, k, :], mv[:, k, :, 1], eps, None, ALU.add).then_inc(rs_mid[k], 1)
                pool.wait_ge(rs_mid[k], c + 1)
                nc.gpsimd.tensor_tensor(out=rs[:, k, :], in0=rs[:, k, :], in1=half_power[:, :], op=ALU.pow).then_inc(rs_ready[k], 1)

            def body(c, slot):
                if exists(c, 1):
                    root(0, c + 1, 4 * EPS)
                if exists(c, 2):
                    gate(c + 2, slot)
                root(1, c, EPS)

            nc.gpsimd.memset(ident[:, :], 0.0).then_inc(made, 1)
            nc.gpsimd.memset(half_power[:, :], -0.5)
            for e in range(NR):
                nc.gpsimd.memset(first_key[:, :, e], 16.0 - e)
            pool.wait_ge(made, 1)
            nc.gpsimd.affine_select(out=ident[:, :], in_=ident[:, :], compare_op=ALU.not_equal, fill=1.0,
                                    base=0, pattern=[[-1, P]], channel_multiplier=1).then_inc(made, 1)
            gate(0, 0)
            root(0, 0, 4 * EPS)
            gate(1, 1)
            run(pool, body)

        @block.tensor
        def _(pe):
            def project(c, slot):
                pe.wait_ge(gated, c + 1)
                wait(pe, v_ready, 2 * c)
                for t in range(TT):
                    for k in range(CT):
                        last = nc.tensor.matmul(pO[t // 2][:, (t % 2) * DM:(t % 2 + 1) * DM], yf[:, slot, k, t * P:(t + 1) * P], w_out[:, k, :],
                                                start=(k == 0), stop=(k == CT - 1))
                    if t % 2:
                        last.then_inc(proj_ready, 1)

            def transpose(c, slot):
                pe.wait_ge(norm_ready[0], c + 1)
                wait(pe, cwT_taken, c)
                for k in range(KC):
                    for t in range(TT):
                        last = nc.tensor.transpose(pT[k][:, t * P:(t + 1) * P], v[:, slot, t, k * P:(k + 1) * P], ident[:, :])
                    last.then_inc(x1T_ready, 1)

            def router(c, slot):
                pe.wait_ge(x1T_taken, 2 * c + 2)
                for t in range(TT):
                    for k in range(KC):
                        last = nc.tensor.matmul(pG[:, t * NR:(t + 1) * NR], x1T[:, slot, k, t * P:(t + 1) * P], w_gate[:, k, :],
                                                start=(k == 0), stop=(k == KC - 1))
                last.then_inc(gate_ready, 1)

            def free(c, m):
                if m >= BANKS:
                    pe.wait_ge(added, ADDS * c + adds_until(m - BANKS))
                elif not (isinstance(c, int) and c == 0):
                    pe.wait_ge(added, ADDS * (c - 1) + adds_until(m - BANKS + ITEMS))

            def pairs(c, slot, t, which=range(EP)):
                for e in which:
                    m = (t // 2) * (ITEMS // 2) + (t % 2) * EP + e
                    free(c, m)
                    for k in range(KC):
                        last = nc.tensor.matmul(pE[m % BANKS][:, :], x1T[:, slot, k, t * P:(t + 1) * P], w_exp[:, k, e * 2 * DM:(e + 1) * 2 * DM],
                                                start=(k == 0), stop=(k == KC - 1))
                    last.then_inc(item_ready, 1)

            def biases(c, half):
                m = half * (ITEMS // 2) + BIAS_ITEM
                pe.wait_ge(cwT_taken, c + 1)
                free(c, m)
                for t in (0, 1):
                    at = (2 * half + t) * P
                    last = nc.tensor.matmul(pE[m % BANKS][:, t * DM:(t + 1) * DM], cwT[:, at:at + P], b_exp[:, :], start=True, stop=True)
                last.then_inc(item_ready, 1)

            def body(c, slot):
                more = exists(c, 1)
                if more:
                    project(c + 1, 1 - slot)
                pairs(c, slot, 0)
                pe.wait_ge(router_step, LINKS * (c + 1))
                for t in range(TT):
                    last = nc.tensor.transpose(pT[0][0:NE, t * P:(t + 1) * P], cw[:, slot, t, 0:NE], ident[:, :])
                last.then_inc(cwT_ready, 1)
                pairs(c, slot, 1)
                if more:
                    transpose(c + 1, 1 - slot)
                biases(c, 0)
                pairs(c, slot, 2, range(0, 1))
                if more:
                    router(c + 1, 1 - slot)
                pairs(c, slot, 2, range(1, EP))
                pairs(c, slot, 3)
                biases(c, 1)

            pe.wait_ge(w_loaded, 16 * (4 + NE))
            pe.wait_ge(made, 2)
            project(0, 0)
            transpose(0, 0)
            router(0, 0)
            run(pe, body)

        @block.scalar
        def _(act):
            def head(c, slot):
                for k in range(KC):
                    act.wait_ge(x1T_ready, 2 * c + k + 1)
                    nc.scalar.activation(x1T[:, slot, k, :], pT[k][:, :], ACT.Copy).then_inc(x1T_taken, 1)
                act.wait_ge(lg_ready, c + 1)
                nc.scalar.activation(pr[:, :, :], lg[:, :, :], ACT.Exp).then_inc(pr_ready, 1)

            def body(c, slot):
                act.wait_ge(cwT_ready, c + 1)
                wait(act, item_ready, ITEMS * c)
                nc.scalar.activation(cwT[:, :], pT[0][0:NE, :], ACT.Copy).then_inc(cwT_taken, 1)
                if exists(c, 1):
                    head(c + 1, 1 - slot)

            head(0, 0)
            run(act, body)

        @block.vector
        def _(dve):
            def residual(c, slot):
                for k in (0, 1):
                    dve.wait_ge(proj_ready, 2 * c + k + 1)
                    if k == 0 and not (isinstance(c, int) and c < 2):
                        dve.wait_ge(norm_ready[1], c - 1)
                    nc.vector.scalar_tensor_tensor(out=v[:, slot, 2 * k:2 * k + 2, :], in0=xr[:, slot, 2 * k:2 * k + 2, :], scalar=4.0,
                                                   in1=pO[k][:, :].rearrange("p (t e) -> p t e", e=DM), op0=ALU.mult, op1=ALU.add).then_inc(v_ready, 1)
                dve.wait_ge(v_ready, 2 * c + 2)

            def moments(k, c, slot):
                for t in range(TT):
                    last = nc.vector.bn_stats(stats[:, k, t, :], v[:, slot, t, :])
                last.then_inc(stat_ready[k], 1)
                hold(dve, stat_ready[k], c + 1, spare2)
                for t in range(TT):
                    last = nc.vector.bn_aggr(mv[:, k, t, :], stats[:, k, t, :])
                last.then_inc(mv_ready[k], 1)

            def norm(k, c, slot, dst):
                dve.wait_ge(rs_ready[k], c + 1)
                if k == 1:
                    dve.wait_ge(result_free[slot], 8 * (c - slot) + 16)
                for t in range(TT):
                    last = nc.vector.tensor_scalar(dst[:, slot, t, :], v[:, slot, t, :], mv[:, k, t, 0:1], rs[:, k, t:t + 1], ALU.subtract, ALU.mult)
                last.then_inc(norm_ready[k], 1)

            def over(col):
                return red[:, col, :].unsqueeze(2).to_broadcast([P, TT, NR])

            def logits(c):
                dve.wait_ge(gate_ready, c + 1)
                nc.vector.tensor_tensor(out=lg[:, :, :], in0=pG[:, 0:TT * NR].rearrange("p (t e) -> p t e", e=NR),
                                        in1=b_gate[:, :].unsqueeze(1).to_broadcast([P, TT, NR]), op=ALU.add).then_inc(router_step, 1)
                dve.wait_ge(router_step, LINKS * c + 1)
                nc.vector.tensor_reduce(red[:, 0, :], lg[:, :, :], AX.X, ALU.max).then_inc(router_step, 1)
                dve.wait_ge(router_step, LINKS * c + 2)
                nc.vector.tensor_tensor(out=lg[:, :, :], in0=lg[:, :, :], in1=over(0), op=ALU.subtract).then_inc(lg_ready, 1)

            def weights(c, slot, stage):
                taken = (2, 5, 10, 16, LINKS)[stage]

                def after(steps):
                    dve.wait_ge(router_step, LINKS * c + steps)

                def largest(src, hot, steps):
                    after(steps)
                    nc.vector.tensor_reduce(red[:, 2, :], src[:, :, :], AX.X, ALU.max).then_inc(router_step, 1)
                    after(steps + 1)
                    nc.vector.tensor_tensor(out=key[:, :, :], in0=src[:, :, :], in1=over(2), op=ALU.is_equal).then_inc(router_step, 1)
                    after(steps + 2)
                    nc.vector.tensor_tensor(out=key[:, :, :], in0=key[:, :, :], in1=first_key[:, :, :], op=ALU.mult).then_inc(router_step, 1)
                    after(steps + 3)
                    nc.vector.tensor_reduce(red[:, 3, :], key[:, :, :], AX.X, ALU.max).then_inc(router_step, 1)
                    after(steps + 4)
                    nc.vector.tensor_tensor(out=hot[:, :, :], in0=key[:, :, :], in1=over(3), op=ALU.is_equal).then_inc(router_step, 1)

                if stage == 0:
                    dve.wait_ge(pr_ready, c + 1)
                    nc.vector.tensor_reduce(red[:, 1, :], pr[:, :, :], AX.X, ALU.add).then_inc(router_step, 1)
                    after(taken + 1)
                    nc.vector.reciprocal(red[:, 1, :], red[:, 1, :]).then_inc(router_step, 1)
                    after(taken + 2)
                    nc.vector.tensor_tensor(out=pr[:, :, :], in0=pr[:, :, :], in1=over(1), op=ALU.mult).then_inc(router_step, 1)
                if stage == 1:
                    largest(pr, hot1, taken)
                if stage == 2:
                    after(taken)
                    nc.vector.scalar_tensor_tensor(out=left[:, :, :], in0=hot1[:, :, :], scalar=-2.0, in1=pr[:, :, :], op0=ALU.mult, op1=ALU.add).then_inc(router_step, 1)
                    largest(left, hot2, taken + 1)
                if stage == 3:
                    after(taken)
                    nc.vector.tensor_tensor(out=hot1[:, :, :], in0=hot1[:, :, :], in1=hot2[:, :, :], op=ALU.add).then_inc(router_step, 1)
                    after(taken + 1)
                    nc.vector.tensor_tensor(out=cw[:, slot, :, :], in0=pr[:, :, :], in1=hot1[:, :, :], op=ALU.mult).then_inc(router_step, 1)
                    after(taken + 2)
                    nc.vector.tensor_reduce(red[:, 4, :], cw[:, slot, :, 0:NE], AX.X, ALU.add).then_inc(router_step, 1)
                    after(taken + 3)
                    nc.vector.tensor_scalar(red[:, 5, :], red[:, 4, :], 0.0, None, ALU.is_le).then_inc(router_step, 1)
                    after(taken + 4)
                    nc.vector.tensor_tensor(out=red[:, 4, :], in0=red[:, 4, :], in1=red[:, 5, :], op=ALU.add).then_inc(router_step, 1)
                    after(taken + 5)
                    nc.vector.reciprocal(red[:, 4, :], red[:, 4, :]).then_inc(router_step, 1)
                    after(taken + 6)
                    nc.vector.tensor_tensor(out=cw[:, slot, :, :], in0=cw[:, slot, :, :], in1=over(4), op=ALU.mult).then_inc(router_step, 1)

            def add_pairs(c, slot, t, which=range(EP)):
                for e in range(2 * which[0], 2 * which[-1] + 2):
                    m = (t // 2) * (ITEMS // 2) + (t % 2) * EP + e // 2
                    done = adds_until(m) - 2 + e % 2
                    dve.wait_ge(item_ready, ITEMS * c + m + 1)
                    if done:
                        dve.wait_ge(added, ADDS * c + done)
                    nc.vector.scalar_tensor_tensor(out=v[:, slot, t, :], in0=pE[m % BANKS][:, (e % 2) * DM:(e % 2 + 1) * DM],
                                                   scalar=cw[:, slot, t, e:e + 1], in1=v[:, slot, t, :], op0=ALU.mult, op1=ALU.add).then_inc(added, 1)

            def add_biases(c, slot, half):
                m = half * (ITEMS // 2) + BIAS_ITEM
                dve.wait_ge(item_ready, ITEMS * c + m + 1)
                dve.wait_ge(added, ADDS * c + adds_until(m) - 1)
                both = v[:, slot, 2 * half:2 * half + 2, :]
                nc.vector.tensor_tensor(out=both, in0=both, in1=pE[m % BANKS][:, :].rearrange("p (t e) -> p t e", e=DM), op=ALU.add).then_inc(added, 1)

            def body(c, slot):
                more = exists(c, 1)
                if more:
                    residual(c + 1, 1 - slot)
                    moments(0, c + 1, 1 - slot)
                add_pairs(c, slot, 0)
                if more:
                    norm(0, c + 1, 1 - slot, v)
                add_pairs(c, slot, 1)
                add_biases(c, slot, 0)
                add_pairs(c, slot, 2, range(0, 3))
                if more:
                    logits(c + 1)
                add_pairs(c, slot, 2, range(3, EP))
                for e in range(EP):
                    if more:
                        weights(c + 1, 1 - slot, e)
                    add_pairs(c, slot, 3, range(e, e + 1))
                add_biases(c, slot, 1)
                dve.wait_ge(added, ADDS * (c + 1))
                moments(1, c, slot)
                norm(1, c, slot, result)

            dve.wait_ge(made, 2)
            dve.wait_ge(w_loaded, 16 * (4 + NE))
            residual(0, 0)
            moments(0, 0, 0)
            norm(0, 0, 0, v)
            logits(0)
            for stage in range(4):
                weights(0, 0, stage)
            run(dve, body)


def kernel(**inputs):
    import numpy as np
    import concourse.bacc as bacc
    from concourse.bass_utils import run_bass_kernel_spmd as launch

    def channels(w):
        return np.ascontiguousarray(np.swapaxes(w.reshape((-1, P) + w.shape[1:]), 0, 1))

    a = {k.replace("L0_attn_", "").replace("L0_ffn_", ""): np.asarray(v) for k, v in inputs.items()}
    both = lambda name, f: np.stack([f(a[name + "_f"]), f(a[name + "_b"])])
    arrays = {
        "x": np.ascontiguousarray(a["x"].reshape(B * L, DM)),
        "in_w": np.ascontiguousarray(a["in_proj_w"].T),
        "out_w": np.ascontiguousarray(a["out_proj_w"].T),
        "norm_w": channels(a["norm_w"]),
        "conv_w": both("conv_w", lambda w: channels(w[:, 0, :])),
        "conv_b": both("conv_b", channels),
        "xproj_w": both("xproj_w", lambda w: np.ascontiguousarray(w.T)),
        "dt_w": both("dtproj_w", lambda w: np.ascontiguousarray(w.T)),
        "dt_b": both("dtproj_b", channels),
        "a_log": both("A_log", channels),
        "d_skip": both("D", channels),
        "gate_w": np.ascontiguousarray(a["gate_w"].T),
        "gate_b": a["gate_b"],
        "expert_w": a["expert_w"],
        "expert_b": a["expert_b"],
    }
    nc = bacc.Bacc("TRN2", target_bir_lowering=False, num_devices=1)
    aps = {k: nc.dram_tensor(f"in_{k}", v.shape, mybir.dt.from_np(v.dtype), kind="ExternalInput").ap() for k, v in arrays.items()}
    out = nc.dram_tensor("out", (B * L, DM), mybir.dt.float32, kind="ExternalOutput").ap()
    mamba_moe(nc, out=out, **aps)
    r = launch(nc, [{f"in_{k}": v for k, v in arrays.items()}], core_ids=[0])
    return r.results[0]["out"].reshape(B, L, DM)
```
